# Optimizing a Trainium2 kernel written in Bass

```python
import numpy as np
import jax
import jax.numpy as jnp

def _softmax(x, axis=-1):
    return jax.nn.softmax(x, axis=axis)
def _gelu(x):
    return jax.nn.gelu(x, approximate=True)
def _silu(x):
    return jax.nn.silu(x)
def _sigmoid(x):
    return jax.nn.sigmoid(x)
def _layernorm(x, axis=-1, eps=1e-5):
    m = jnp.mean(x, axis=axis, keepdims=True)
    v = jnp.var(x, axis=axis, keepdims=True)
    return (x - m) / jnp.sqrt(v + eps)
def _scatter_add(tgt, idx, src, axis=0):
    return tgt.at[idx].add(src)
def _segment_sum(src, seg, n):
    return jax.ops.segment_sum(src, seg, n)

kernel_name = 'mk_metaformer_d2_conv_nhwc128_95fe2a'

def setup_inputs(seed: int = 0):
    np.random.seed(seed)
    _w = jnp.asarray
    def _rec_inputs():
        import jax
        import jax.numpy as jnp
        _gk = jax.random.key(seed)
        x = 7.22e-05 + 1 * jax.random.normal(jax.random.fold_in(_gk, 1), (1, 256, 256, 128), jnp.float32)
        return x
    x = _rec_inputs()
    def _L0_conv_setup():
        import jax, jax.numpy as jnp
        import numpy as np
        C_Z = 128
        N_HEADS = 4
        HEAD_DIM = 32
        TOTAL = N_HEADS * HEAD_DIM
        B, N = (1, 256)
        key = jax.random.key(seed)
        ks = jax.random.split(key, 10)
        s = lambda k, sh: jax.random.normal(k, sh, dtype=jnp.float32) * 0.02
        return {'pair_representation': jax.random.normal(ks[0], (B, N, N, C_Z), dtype=jnp.float32), 'ln_gamma': jnp.ones((C_Z,), jnp.float32), 'ln_beta': jnp.zeros((C_Z,), jnp.float32), 'Wq': s(ks[1], (C_Z, TOTAL)), 'Wk': s(ks[2], (C_Z, TOTAL)), 'Wv': s(ks[3], (C_Z, TOTAL)), 'Wb': s(ks[4], (C_Z, N_HEADS)), 'Wg': s(ks[5], (C_Z, TOTAL)), 'bg': jnp.zeros((TOTAL,), jnp.float32), 'Wo': s(ks[6], (TOTAL, C_Z)), 'bo': jnp.zeros((C_Z,), jnp.float32)}
    _L0_conv_all = _L0_conv_setup()
    _L0_conv_in = {k: v for k, v in _L0_conv_all.items() if k in ('ln_gamma', 'ln_beta', 'Wq', 'Wk', 'Wv', 'Wb', 'Wg', 'bg', 'Wo', 'bo', )}
    del _L0_conv_all

    def _L0_ffn_setup():
        import jax, jax.numpy as jnp
        import numpy as np
        BN_EPS = 1e-05
        key = jax.random.key(seed)
        k1, k2, k3 = jax.random.split(key, 3)
        B, T, I, H = (64, 2048, 128, 128)
        x = jax.random.normal(k1, (B, T, I), dtype=jnp.float32)
        W = jax.random.normal(k2, (H, I), dtype=jnp.float32) * (1.0 / np.sqrt(I))
        V = jnp.linalg.qr(jax.random.normal(k3, (H, H), dtype=jnp.float32))[0]
        gamma = jnp.ones((H,), dtype=jnp.float32)
        beta = jnp.zeros((H,), dtype=jnp.float32)
        return {'x': x, 'W': W, 'V': V, 'gamma': gamma, 'beta': beta}
    _L0_ffn_all = _L0_ffn_setup()
    _L0_ffn_in = {k: v for k, v in _L0_ffn_all.items() if k in ('W', 'V', 'gamma', 'beta', )}
    del _L0_ffn_all

    def _L1_conv_setup():
        import jax, jax.numpy as jnp
        import numpy as np
        EPS = 1e-05

        def layer_norm(x, g, b):
            mu = jnp.mean(x, axis=-1, keepdims=True)
            var = jnp.mean(jnp.square(x - mu), axis=-1, keepdims=True)
            return (x - mu) * jax.lax.rsqrt(var + EPS) * g + b
        key = jax.random.key(seed)
        ks = jax.random.split(key, 16)
        b, n, dim, hid = (2, 384, 128, 128)
        s_in = 1.0 / np.sqrt(dim)
        s_hid = 1.0 / np.sqrt(hid)
        inp = {'x': jax.random.normal(ks[0], (b, n, n, dim), jnp.float32), 'norm_g': jnp.ones((dim,), jnp.float32), 'norm_b': jnp.zeros((dim,), jnp.float32), 'left_w': jax.random.normal(ks[1], (dim, hid), jnp.float32) * s_in, 'left_b': jnp.zeros((hid,), jnp.float32), 'right_w': jax.random.normal(ks[2], (dim, hid), jnp.float32) * s_in, 'right_b': jnp.zeros((hid,), jnp.float32), 'lgate_w': jax.random.normal(ks[3], (dim, hid), jnp.float32) * s_in * 0.1, 'lgate_b': jnp.ones((hid,), jnp.float32), 'rgate_w': jax.random.normal(ks[4], (dim, hid), jnp.float32) * s_in * 0.1, 'rgate_b': jnp.ones((hid,), jnp.float32), 'ogate_w': jax.random.normal(ks[5], (dim, hid), jnp.float32) * s_in * 0.1, 'ogate_b': jnp.ones((hid,), jnp.float32), 'onorm_g': jnp.ones((hid,), jnp.float32), 'onorm_b': jnp.zeros((hid,), jnp.float32), 'to_out_w': jax.random.normal(ks[6], (hid, dim), jnp.float32) * s_hid, 'to_out_b': jnp.zeros((dim,), jnp.float32)}
        return inp
    _L1_conv_all = _L1_conv_setup()
    _L1_conv_in = {k: v for k, v in _L1_conv_all.items() if k in ('norm_g', 'norm_b', 'left_w', 'left_b', 'right_w', 'right_b', 'lgate_w', 'lgate_b', 'rgate_w', 'rgate_b', 'ogate_w', 'ogate_b', 'onorm_g', 'onorm_b', 'to_out_w', 'to_out_b', )}
    del _L1_conv_all

    def _L1_ffn_setup():
        import jax, jax.numpy as jnp
        import numpy as np
        B, N, D, C, E, K = (8, 8192, 128, 128, 8, 2)
        key = jax.random.key(seed)
        k0, k1, k2 = jax.random.split(key, 3)
        x = jax.random.normal(k0, (B, N, D), dtype=jnp.float32)
        router_w = jax.random.normal(k1, (D, E), dtype=jnp.float32) * 0.05
        router_b = jnp.zeros((E,), dtype=jnp.float32)
        expert_w = jax.random.normal(k2, (E, D, C), dtype=jnp.float32) * (1.0 / np.sqrt(D))
        expert_b = jnp.zeros((E, C), dtype=jnp.float32)
        return {'x': x, 'router_w': router_w, 'router_b': router_b, 'expert_w': expert_w, 'expert_b': expert_b}
    _L1_ffn_all = _L1_ffn_setup()
    _L1_ffn_in = {k: v for k, v in _L1_ffn_all.items() if k in ('router_w', 'router_b', 'expert_w', 'expert_b', )}
    del _L1_ffn_all

    return {
        "x": x,
        "L0_conv_ln_gamma": _L0_conv_in["ln_gamma"],
        "L0_conv_ln_beta": _L0_conv_in["ln_beta"],
        "L0_conv_Wq": _L0_conv_in["Wq"],
        "L0_conv_Wk": _L0_conv_in["Wk"],
        "L0_conv_Wv": _L0_conv_in["Wv"],
        "L0_conv_Wb": _L0_conv_in["Wb"],
        "L0_conv_Wg": _L0_conv_in["Wg"],
        "L0_conv_bg": _L0_conv_in["bg"],
        "L0_conv_Wo": _L0_conv_in["Wo"],
        "L0_conv_bo": _L0_conv_in["bo"],
        "L0_ffn_W": _L0_ffn_in["W"],
        "L0_ffn_V": _L0_ffn_in["V"],
        "L0_ffn_gamma": _L0_ffn_in["gamma"],
        "L0_ffn_beta": _L0_ffn_in["beta"],
        "L1_conv_norm_g": _L1_conv_in["norm_g"],
        "L1_conv_norm_b": _L1_conv_in["norm_b"],
        "L1_conv_left_w": _L1_conv_in["left_w"],
        "L1_conv_left_b": _L1_conv_in["left_b"],
        "L1_conv_right_w": _L1_conv_in["right_w"],
        "L1_conv_right_b": _L1_conv_in["right_b"],
        "L1_conv_lgate_w": _L1_conv_in["lgate_w"],
        "L1_conv_lgate_b": _L1_conv_in["lgate_b"],
        "L1_conv_rgate_w": _L1_conv_in["rgate_w"],
        "L1_conv_rgate_b": _L1_conv_in["rgate_b"],
        "L1_conv_ogate_w": _L1_conv_in["ogate_w"],
        "L1_conv_ogate_b": _L1_conv_in["ogate_b"],
        "L1_conv_onorm_g": _L1_conv_in["onorm_g"],
        "L1_conv_onorm_b": _L1_conv_in["onorm_b"],
        "L1_conv_to_out_w": _L1_conv_in["to_out_w"],
        "L1_conv_to_out_b": _L1_conv_in["to_out_b"],
        "L1_ffn_router_w": _L1_ffn_in["router_w"],
        "L1_ffn_router_b": _L1_ffn_in["router_b"],
        "L1_ffn_expert_w": _L1_ffn_in["expert_w"],
        "L1_ffn_expert_b": _L1_ffn_in["expert_b"],
    }

def reference(x, L0_conv_ln_gamma, L0_conv_ln_beta, L0_conv_Wq, L0_conv_Wk, L0_conv_Wv, L0_conv_Wb, L0_conv_Wg, L0_conv_bg, L0_conv_Wo, L0_conv_bo, L0_ffn_W, L0_ffn_V, L0_ffn_gamma, L0_ffn_beta, L1_conv_norm_g, L1_conv_norm_b, L1_conv_left_w, L1_conv_left_b, L1_conv_right_w, L1_conv_right_b, L1_conv_lgate_w, L1_conv_lgate_b, L1_conv_rgate_w, L1_conv_rgate_b, L1_conv_ogate_w, L1_conv_ogate_b, L1_conv_onorm_g, L1_conv_onorm_b, L1_conv_to_out_w, L1_conv_to_out_b, L1_ffn_router_w, L1_ffn_router_b, L1_ffn_expert_w, L1_ffn_expert_b):
    import jax
    import jax.numpy as jnp
    def _L0_conv_ref(pair_representation, ln_gamma, ln_beta, Wq, Wk, Wv, Wb, Wg, bg, Wo, bo):
        import jax, jax.numpy as jnp
        import numpy as np
        C_Z = 128
        N_HEADS = 4
        HEAD_DIM = 32
        TOTAL = N_HEADS * HEAD_DIM
        B, N = (1, 256)
        x = pair_representation
        mu = jnp.mean(x, axis=-1, keepdims=True)
        var = jnp.mean((x - mu) ** 2, axis=-1, keepdims=True)
        x = (x - mu) * jax.lax.rsqrt(var + 1e-05) * ln_gamma + ln_beta
        b, n, _, _ = x.shape
        split = lambda t: t.reshape(b, n, n, N_HEADS, HEAD_DIM)
        Q = split(x @ Wq)
        K = split(x @ Wk)
        V = split(x @ Wv)
        G = jax.nn.sigmoid(split(x @ Wg + bg))
        Bias = x @ Wb
        scores = jnp.einsum('bijhd,bikhd->bijkh', Q, K) / np.float32(np.sqrt(HEAD_DIM))
        scores = scores + Bias[:, None]
        attn = jax.nn.softmax(scores, axis=3)
        vals = jnp.einsum('bijkh,bikhd->bijhd', attn, V)
        vals = (G * vals).reshape(b, n, n, TOTAL)
        return vals @ Wo + bo

    def _L0_ffn_ref(x, W, V, gamma, beta):
        import jax, jax.numpy as jnp
        import numpy as np
        BN_EPS = 1e-05
        B, T, H = (x.shape[0], x.shape[1], W.shape[0])
        Wx = jnp.einsum('bti,hi->bth', x, W)
        flat = Wx.reshape(B * T, H)
        mean = jnp.mean(flat, axis=0)
        var = jnp.var(flat, axis=0)
        Wx = ((flat - mean) * jax.lax.rsqrt(var + BN_EPS) * gamma + beta).reshape(B, T, H)
        Vt = V.T

        def step(yt, wx_t):
            yt = jax.nn.sigmoid(wx_t + yt @ Vt)
            return (yt, yt)
        y0 = jnp.zeros((B, H), dtype=Wx.dtype)
        _, ys = jax.lax.scan(step, y0, jnp.swapaxes(Wx, 0, 1))
        return jnp.swapaxes(ys, 0, 1)

    def _L1_conv_ref(x, norm_g, norm_b, left_w, left_b, right_w, right_b, lgate_w, lgate_b, rgate_w, rgate_b, ogate_w, ogate_b, onorm_g, onorm_b, to_out_w, to_out_b):
        import jax, jax.numpy as jnp
        import numpy as np
        EPS = 1e-05

        def layer_norm(x, g, b):
            mu = jnp.mean(x, axis=-1, keepdims=True)
            var = jnp.mean(jnp.square(x - mu), axis=-1, keepdims=True)
            return (x - mu) * jax.lax.rsqrt(var + EPS) * g + b
        xn = layer_norm(x, norm_g, norm_b)
        left = xn @ left_w + left_b
        right = xn @ right_w + right_b
        left = left * jax.nn.sigmoid(xn @ lgate_w + lgate_b)
        right = right * jax.nn.sigmoid(xn @ rgate_w + rgate_b)
        out_gate = jax.nn.sigmoid(xn @ ogate_w + ogate_b)
        out = jnp.einsum('bkjd,bkid->bijd', left, right)
        out = layer_norm(out, onorm_g, onorm_b) * out_gate
        return out @ to_out_w + to_out_b

    def _L1_ffn_ref(x, router_w, router_b, expert_w, expert_b):
        import jax, jax.numpy as jnp
        import numpy as np
        B, N, D, C, E, K = (8, 8192, 128, 128, 8, 2)
        router_probs = jax.nn.softmax(x @ router_w + router_b, axis=-1)
        top_p, top_i = jax.lax.top_k(router_probs, K)
        top_p = top_p / jnp.sum(top_p, axis=-1, keepdims=True)
        expert_out = jnp.einsum('bnd,edc->bnec', x, expert_w) + expert_b
        gathered = jnp.take_along_axis(expert_out, top_i[..., None], axis=2)
        return jnp.einsum('bnk,bnkc->bnc', top_p, gathered)

    def _gn(v, G=32, eps=1e-5):
        B_, H_, W_, C_ = v.shape
        g = v.reshape(B_, H_, W_, G, C_ // G)
        m = jnp.mean(g, axis=(1, 2, 4), keepdims=True)
        s = jnp.var(g, axis=(1, 2, 4), keepdims=True)
        return ((g - m) / jnp.sqrt(s + eps)).reshape(v.shape)

    def _ln_c(v, eps=1e-6):
        m = jnp.mean(v, axis=-1, keepdims=True)
        s = jnp.var(v, axis=-1, keepdims=True)
        return (v - m) / jnp.sqrt(s + eps)

    def _ln_t(v, eps=1e-5):
        m = jnp.mean(v, axis=-1, keepdims=True)
        s = jnp.var(v, axis=-1, keepdims=True)
        return (v - m) / jnp.sqrt(s + eps)

    def _to_tokens(v):
        B_, H_, W_, C_ = v.shape
        return v.reshape(B_, H_ * W_, C_)
    def _from_tokens(t, like):
        return t.reshape(like.shape)

    x = x + _L0_conv_ref(_ln_c(x), L0_conv_ln_gamma, L0_conv_ln_beta, L0_conv_Wq, L0_conv_Wk, L0_conv_Wv, L0_conv_Wb, L0_conv_Wg, L0_conv_bg, L0_conv_Wo, L0_conv_bo)
    t = _to_tokens(x)
    t = t + _L0_ffn_ref(_ln_t(t), L0_ffn_W, L0_ffn_V, L0_ffn_gamma, L0_ffn_beta)
    x = _from_tokens(t, x)
    x = x + _L1_conv_ref(_ln_c(x), L1_conv_norm_g, L1_conv_norm_b, L1_conv_left_w, L1_conv_left_b, L1_conv_right_w, L1_conv_right_b, L1_conv_lgate_w, L1_conv_lgate_b, L1_conv_rgate_w, L1_conv_rgate_b, L1_conv_ogate_w, L1_conv_ogate_b, L1_conv_onorm_g, L1_conv_onorm_b, L1_conv_to_out_w, L1_conv_to_out_b)
    t = _to_tokens(x)
    t = t + _L1_ffn_ref(_ln_t(t), L1_ffn_router_w, L1_ffn_router_b, L1_ffn_expert_w, L1_ffn_expert_b)
    x = _from_tokens(t, x)
    return x


_drawn_inputs = setup_inputs


def setup_inputs(seed=0):
    import zlib

    import numpy as np

    out = dict(_drawn_inputs(seed))
    spreads = {'L0_conv_ln_gamma': (1.0, 0.6),
     'L0_conv_ln_beta': (0.0, 0.267),
     'L0_conv_bg': (0.0, 0.8),
     'L0_conv_bo': (0.0, 0.1),
     'L0_ffn_gamma': (1.0, 0.2),
     'L0_ffn_beta': (0.0, 0.1),
     'L1_conv_norm_g': (1.0, 0.2),
     'L1_conv_norm_b': (0.0, 0.1),
     'L1_conv_left_b': (0.0, 0.1),
     'L1_conv_right_b': (0.0, 0.1),
     'L1_conv_lgate_b': (1.0, 0.2),
     'L1_conv_rgate_b': (1.0, 0.2),
     'L1_conv_ogate_b': (1.0, 0.2),
     'L1_conv_onorm_g': (1.0, 0.2),
     'L1_conv_onorm_b': (0.0, 0.1),
     'L1_conv_to_out_b': (0.0, 0.1),
     'L1_ffn_router_b': (0.0, 0.1),
     'L1_ffn_expert_b': (0.0, 0.1)}
    factors = {'L0_conv_Wq': 8.0, 'L0_conv_Wk': 8.0, 'L0_conv_Wb': 8.0, 'L0_conv_Wg': 8.0}
    for name, (base, spread) in spreads.items():
        noise = np.random.default_rng([zlib.crc32(name.encode()), seed]).standard_normal(out[name].shape)
        drawn = base * np.exp(spread * noise) if base else spread * noise
        out[name] = jnp.asarray(drawn.astype(out[name].dtype))
    for name, factor in factors.items():
        out[name] = (out[name] * factor).astype(out[name].dtype)
    return out
```

```python
import numpy as np
import concourse.bass as bass
from concourse import mybir
from contextlib import ExitStack

F32 = mybir.dt.float32
I32 = mybir.dt.int32
ALU = mybir.AluOpType
ACT = mybir.ActivationFunctionType
AX = mybir.AxisListType

P = 128
C = 128
ROWS = COLS = 256
TOKENS = ROWS * COLS
HEADS, HEAD_DIM = 4, 32
TILES = 8
UNIT = TILES * P
UNITS = TOKENS // UNIT
BANK = 512
PITCH = TOKENS + 1024
EPS_C, EPS_LN, EPS_T, EPS_BN = 1e-6, 1e-5, 1e-5, 1e-5
EXPERTS = 8
LOWEST = -3.0e38
AHEAD = 4


def each_unit(eng, units, slots, step):
    for s in range(slots):
        step(s, s)
    with eng.Fori(slots, units - slots, slots) as u:
        for s in range(slots):
            step(u + s if s else u, s)
    for s in range(slots):
        step(units - slots + s, s)


def exists(u, units):
    return not isinstance(u, int) or 0 <= u < units


def wait_count(eng, sem, n):
    if not isinstance(n, int) or n > 0:
        eng.wait_ge(sem, n)


def wait_alone(eng, sem, n, over, over_n):
    if isinstance(n, int):
        wait_count(eng, sem, n)
    else:
        value = eng.snap(n)
        eng.wait_ge(over, over_n)
        eng.wait_ge(sem, value)


def wait_unit(eng, sem, u, per=1, part=None):
    if not isinstance(u, int) or u >= 0:
        wait_count(eng, sem, u * per + (per if part is None else part))


def wait_dma(eng, sems, u, slot, slots=2):
    if not isinstance(u, int) or u >= 0:
        eng.wait_ge(sems[slot], (u - slot) * (16 // slots) + 16)


class Memory:

    def __init__(self, nc, stack, stage):
        self.nc, self.stack, self.stage, self.used = nc, stack, stage, []

    def sbuf(self, name, shape, dtype=F32):
        return self.stack.enter_context(self.nc.sbuf_tensor(f"{self.stage}_{name}", shape, dtype))

    def psum(self, name, shape):
        return self.stack.enter_context(self.nc.psum_tensor(f"{self.stage}_{name}", shape, F32))

    def sem(self, name):
        sem = self.stack.enter_context(self.nc.semaphore(f"{self.stage}_{name}"))
        self.used.append(sem)
        return sem

    def clear(self):
        with self.nc.Block() as block:
            @block.gpsimd
            def _(pool):
                for sem in self.used:
                    pool.sem_clear(sem)

    def sems(self, name, n=2):
        return [self.sem(f"{name}{i}") for i in range(n)]


def column(vector):
    return vector.rearrange("(c a) -> c a", a=1)


def row_to_all(vector, n=P):
    return vector.rearrange("(a c) -> a c", a=1).to_broadcast([n, vector.shape[0]])


def tile_stats(nc, stats, x, done):
    for t in range(TILES):
        last = nc.vector.bn_stats(stats[:, t, :], x[:, t, :])
    last.then_inc(done, 1)


class RowNorm:

    def __init__(self, mem, a, b):
        self.a, self.b = a, b
        self.stats = [mem.sbuf(f"stats{s}", [P, TILES, 6]) for s in range(2)]
        self.mean = [mem.sbuf(f"mean{s}", [P, TILES]) for s in range(2)]
        self.rstd = [mem.sbuf(f"rstd{s}", [P, TILES]) for s in range(2)]
        self.tmp = [mem.sbuf(f"normtmp{i}", [P, TILES]) for i in range(6)]
        self.power = mem.sbuf("power", [P, TILES])
        self.quarter = mem.sbuf("quarter", [P, TILES])
        self.step_done = mem.sem("norm_step")

    def prepare(self, nc):
        nc.gpsimd.memset(self.quarter[:], self.a / 4)
        nc.gpsimd.memset(self.power[:], -0.5).then_inc(self.step_done, 1)
        nc.gpsimd.wait_ge(self.step_done, 1)

    def rstd_of(self, nc, u, s, ready):
        g, t = nc.gpsimd, self.tmp
        count_e = self.stats[s]
        mean_even, dev_even = count_e[:, :, 1], count_e[:, :, 2]
        mean_odd, dev_odd = count_e[:, :, 4], count_e[:, :, 5]
        base = u * 4 + 1
        wait_unit(g, ready, u - 1)
        g.tensor_tensor(t[0][:], mean_even, mean_odd, ALU.add)
        g.tensor_tensor(t[1][:], mean_even, mean_odd, ALU.subtract)
        g.tensor_tensor(t[2][:], dev_even, dev_odd, ALU.add).then_inc(self.step_done, 1)
        g.wait_ge(self.step_done, base + 1)
        g.tensor_tensor(t[3][:], t[1][:], t[1][:], ALU.mult)
        g.tensor_scalar(self.mean[s][:], t[0][:], 0.5, 0.0, ALU.mult, ALU.add)
        g.tensor_scalar(t[4][:], t[2][:], self.a / C, self.b, ALU.mult, ALU.add).then_inc(self.step_done, 1)
        g.wait_ge(self.step_done, base + 2)
        g.tensor_tensor(t[5][:], t[3][:], self.quarter[:], ALU.mult).then_inc(self.step_done, 1)
        g.wait_ge(self.step_done, base + 3)
        g.tensor_tensor(t[0][:], t[4][:], t[5][:], ALU.add).then_inc(self.step_done, 1)
        g.wait_ge(self.step_done, base + 4)
        g.tensor_tensor(self.rstd[s][:], t[0][:], self.power[:], ALU.pow).then_inc(ready, 1)

    def apply(self, nc, s, out, x, done):
        for t in range(TILES):
            last = nc.vector.tensor_scalar(out[:, t, :], x[:, t, :], self.mean[s][:, t:t + 1],
                                           self.rstd[s][:, t:t + 1], ALU.subtract, ALU.mult)
        last.then_inc(done, 1)


def make_identity(nc, ident, sem, value=1.0):
    nc.gpsimd.memset(ident[:], 0.0).then_inc(sem, 1)
    nc.gpsimd.wait_ge(sem, 1)
    nc.gpsimd.affine_select(out=ident[:], in_=ident[:], compare_op=ALU.not_equal, fill=value, base=0,
                            pattern=[[-1, P]], channel_multiplier=1).then_inc(sem, 1)


def norm_project(nc, stage, x, weight, gamma, beta, normed, projected, out_rows, a, b, wx_stats=None):
    with ExitStack() as stack:
        mem = Memory(nc, stack, stage)
        norm = RowNorm(mem, a, b)
        x_in = [mem.sbuf(f"x{s}", [P, TILES, C]) for s in range(AHEAD)]
        centred = [mem.sbuf(f"centred{s}", [P, TILES, C]) for s in range(2)]
        xT = [mem.sbuf(f"xT{s}", [C, UNIT]) for s in range(2)]
        result = [mem.sbuf(f"result{s}", [out_rows, UNIT]) for s in range(2)]
        w_raw = mem.sbuf("w_raw", [C, out_rows])
        w = mem.sbuf("w", [C, out_rows])
        ident = mem.sbuf("ident", [P, P])
        g_col, b_col = mem.sbuf("g_col", [C, 1]), mem.sbuf("b_col", [C, 1])
        turned = [mem.psum(f"turned{s}", [C, UNIT]) for s in range(2)]
        product = [mem.psum(f"product{s}", [out_rows, UNIT]) for s in range(2)]
        if wx_stats is not None:
            batch = mem.sbuf("batch", [out_rows, 2 * UNITS, 6])

        weights_in, ident_ready, w_ready, w_turned = (mem.sem(n) for n in ("weights_in", "ident", "w_ready", "w_turned"))
        x_loaded, normed_out, result_out = mem.sems("x_loaded", AHEAD), mem.sems("normed_out"), mem.sems("result_out")
        stats_ready, rstd_ready, centred_ready = (mem.sem(n) for n in ("stats", "rstd", "centred_ready"))
        turned_ready, xT_ready, product_ready, result_ready, batch_ready = (
            mem.sem(n) for n in ("turned_ready", "xT_ready", "product_ready", "result_ready", "batch_ready"))
        loads = 16 * (1 + 2 * (gamma is not None))
        x_units = x.rearrange("(u t p) c -> u p t c", t=TILES, p=P)

        with nc.Block() as block:
            @block.sync
            def _(sp):
                sp.dma_start(w_raw[:], weight).then_inc(weights_in, 16)
                if gamma is not None:
                    sp.dma_start(g_col[:], column(gamma)).then_inc(weights_in, 16)
                    sp.dma_start(b_col[:], column(beta)).then_inc(weights_in, 16)

                def step(u, s):
                    wait_unit(sp, centred_ready, u - AHEAD)
                    sp.dma_start(x_in[s][:], x_units[u]).then_inc(x_loaded[s], 16)

                each_unit(sp, UNITS, AHEAD, step)

            @block.vector
            def _(dve):
                def stats(u, s):
                    wait_dma(dve, x_loaded, u, s, AHEAD)
                    tile_stats(nc, norm.stats[s % 2], x_in[s], stats_ready)

                if wx_stats is not None:
                    dve.wait_ge(w_turned, 1)
                    nc.vector.tensor_copy(w[:], turned[0][:, 0:out_rows]).then_inc(w_ready, 1)
                else:
                    dve.wait_ge(weights_in, loads)
                    nc.vector.tensor_copy(w[:], w_raw[:]).then_inc(w_ready, 1)
                stats(0, 0)

                def batch_stats(u):
                    wait_unit(dve, result_ready, u)
                    s = batch_slot[0]
                    for half in range(2):
                        last = nc.vector.bn_stats(batch[:, bass.ds(u * 2 + half, 1), :],
                                                  result[s][:, half * BANK:(half + 1) * BANK])
                    last.then_inc(batch_ready, 1)

                batch_slot = [0]

                def step(u, s):
                    if exists(u + 1, UNITS):
                        stats(u + 1, (s + 1) % AHEAD)
                    wait_unit(dve, rstd_ready, u)
                    wait_unit(dve, turned_ready, u - 2)
                    norm.apply(nc, s % 2, centred[s % 2], x_in[s], centred_ready)
                    if wx_stats is not None and exists(u - 1, UNITS):
                        batch_slot[0] = (s + 1) % 2
                        batch_stats(u - 1)

                each_unit(dve, UNITS, AHEAD, step)
                if wx_stats is not None:
                    batch_slot[0] = (UNITS - 1) % 2
                    batch_stats(UNITS - 1)
                    dve.wait_ge(batch_ready, UNITS)
                    nc.vector.bn_aggr(wx_stats[:], batch[:].rearrange("p n k -> p (n k)"))

            @block.gpsimd
            def _(pool):
                make_identity(nc, ident, ident_ready)
                norm.prepare(nc)

                def step(u, s):
                    wait_unit(pool, stats_ready, u)
                    wait_unit(pool, centred_ready, u - 2)
                    norm.rstd_of(nc, u, s, rstd_ready)

                each_unit(pool, UNITS, 2, step)

            @block.tensor
            def _(pe):
                pe.wait_ge(ident_ready, 2)
                pe.wait_ge(weights_in, loads)
                if wx_stats is not None:
                    nc.tensor.transpose(turned[0][:, 0:out_rows], w_raw[:], ident[:]).then_inc(w_turned, 1)
                pe.wait_ge(w_ready, 1)

                def multiply(u, s):
                    wait_unit(pe, xT_ready, u)
                    wait_unit(pe, result_ready, u - 2)
                    for half in range(2):
                        cols = slice(half * BANK, (half + 1) * BANK)
                        last = nc.tensor.matmul(product[s][:, cols], w[:], xT[s][:, cols], start=True, stop=True)
                    last.then_inc(product_ready, 1)

                def step(u, s):
                    wait_unit(pe, centred_ready, u)
                    wait_unit(pe, xT_ready, u - 2)
                    for t in range(TILES):
                        last = nc.tensor.transpose(turned[s][:, t * P:(t + 1) * P], centred[s][:, t, :], ident[:])
                    last.then_inc(turned_ready, 1)
                    if exists(u - 1, UNITS):
                        multiply(u - 1, 1 - s)

                each_unit(pe, UNITS, 2, step)
                multiply(UNITS - 1, (UNITS - 1) % 2)

            @block.scalar
            def _(act):
                act.wait_ge(weights_in, loads)
                if wx_stats is not None:
                    act.wait_ge(w_ready, 1)

                def store_result(u, s):
                    wait_unit(act, product_ready, u)
                    wait_dma(act, result_out, u - 2, s)
                    if wx_stats is not None:
                        wait_unit(act, batch_ready, u - 2)
                    for half in range(2):
                        cols = slice(half * BANK, (half + 1) * BANK)
                        last = nc.scalar.copy(result[s][:, cols], product[s][:, cols])
                    last.then_inc(result_ready, 1)
                    wait_unit(act, result_ready, u)
                    act.dma_start(projected(u), result[s][:]).then_inc(result_out[s], 16)


                def step(u, s):
                    wait_unit(act, turned_ready, u)
                    wait_unit(act, product_ready, u - 2)
                    if normed is not None:
                        wait_dma(act, normed_out, u - 2, s)
                    for half in range(2):
                        cols = slice(half * BANK, (half + 1) * BANK)
                        if gamma is not None:
                            last = nc.scalar.activation(xT[s][:, cols], turned[s][:, cols], ACT.Identity,
                                                        scale=g_col[:, 0:1], bias=b_col[:, 0:1])
                        else:
                            last = nc.scalar.copy(xT[s][:, cols], turned[s][:, cols])
                    last.then_inc(xT_ready, 1)
                    if normed is not None:
                        wait_unit(act, xT_ready, u)
                        act.dma_start(normed[bass.ds(u * (UNIT // COLS), UNIT // COLS)].rearrange("r c t -> c r t"),
                                      xT[s][:].rearrange("c (r t) -> c r t", t=COLS)).then_inc(normed_out[s], 16)
                    if exists(u - 1, UNITS):
                        store_result(u - 1, 1 - s)

                each_unit(act, UNITS, 2, step)
                store_result(UNITS - 1, (UNITS - 1) % 2)
                for s in range(2):
                    wait_dma(act, result_out, UNITS - 2 + s, s)
                    if normed is not None:
                        wait_dma(act, normed_out, UNITS - 2 + s, s)

        mem.clear()


def attention(nc, x, normed, pair_bias, Wq, Wk, Wv, Wg, bg, Wo, bo, x1):
    scale = 1.0 / float(np.sqrt(HEAD_DIM))
    with ExitStack() as stack:
        mem = Memory(nc, stack, "att")
        xT = [mem.sbuf(f"xT{s}", [C, COLS]) for s in range(AHEAD)]
        x_res = [mem.sbuf(f"x_res{s}", [P, 2, C]) for s in range(AHEAD)]
        qk = [mem.sbuf(f"qk{s}", [C, 2, COLS]) for s in range(2)]
        v = [mem.sbuf(f"v{s}", [P, 2, C]) for s in range(AHEAD)]
        gate = [mem.sbuf(f"gate{s}", [C, COLS]) for s in range(AHEAD)]
        probs = [mem.sbuf(f"probs{s}", [P, HEADS, 2, COLS]) for s in range(2)]
        top = [mem.sbuf(f"top{s}", [P, HEADS * 2]) for s in range(2)]
        neg_top = [mem.sbuf(f"neg_top{s}", [P, HEADS * 2]) for s in range(2)]
        total = [mem.sbuf(f"total{s}", [P, HEADS * 2]) for s in range(2)]
        inv = [mem.sbuf(f"inv{s}", [P, HEADS * 2]) for s in range(2)]
        probsT = mem.sbuf("probsT", [P, HEADS, 2, COLS])
        gate_inv = mem.sbuf("gate_inv", [C, COLS])
        valuesT = [mem.sbuf(f"valuesT{s}", [C, COLS]) for s in range(2)]
        x_bo = [mem.sbuf(f"x_bo{s}", [P, 2, C]) for s in range(2)]
        x1_out = [mem.sbuf(f"x1_out{s}", [P, 2, C]) for s in range(2)]
        bias = mem.sbuf("bias", [P, HEADS, 2, COLS])
        w = {n: mem.sbuf(f"w_{n}", [C, C]) for n in ("q", "k", "v", "g", "o", "q_raw")}
        bg_col, half_bg, bo_all = mem.sbuf("bg_col", [C, 1]), mem.sbuf("half_bg", [C, 1]), mem.sbuf("bo_all", [P, C])
        wait_tick = mem.sbuf("wait_tick", [P, HEADS])
        ident, half_ident = mem.sbuf("ident", [P, P]), mem.sbuf("half_ident", [P, P])

        scores = [mem.psum(f"scores{h}", [P, 2, COLS]) for h in range(HEADS)]
        bank_a, bank_b, bank_c, bank_d = (mem.psum(f"bank_{n}", [P, 2, COLS]) for n in "abcd")

        weights_in, ident_ready, w_ready = mem.sem("weights_in"), mem.sem("ident"), mem.sem("w_ready")
        xT_loaded, res_loaded, x1_stored = mem.sems("xT_loaded", AHEAD), mem.sems("res_loaded", AHEAD), mem.sems("x1_stored")
        (projected, qk_ready, gv_ready, scored, biased, neg_ready, exp_ready, inv_ready, turned, even_ready,
         odd_ready, inv_turned, gate_inv_ready, valued, valuesT_ready, out_ready, x_bo_ready, x1_ready) = (
            mem.sem(n) for n in ("projected", "qk_ready", "gv_ready", "scored", "biased", "neg_ready", "exp_ready",
                                 "inv_ready", "turned", "even_ready", "odd_ready", "inv_turned", "gate_inv_ready",
                                 "valued", "valuesT_ready", "out_ready", "x_bo_ready", "x1_ready"))
        x_rows = x.rearrange("(i t p) c -> i p t c", t=2, p=P)
        x1_rows = x1.rearrange("(i t p) c -> i p t c", t=2, p=P)
        loads = 16 * 9

        with nc.Block() as block:
            @block.sync
            def _(sp):
                for name, src in (("q_raw", Wq), ("k", Wk), ("v", Wv), ("g", Wg), ("o", Wo)):
                    sp.dma_start(w[name][:], src).then_inc(weights_in, 16)
                sp.dma_start(bg_col[:], column(bg)).then_inc(weights_in, 16)
                sp.dma_start(bo_all[:], row_to_all(bo)).then_inc(weights_in, 16)
                for t in range(2):
                    sp.dma_start(bias[:, :, t, :], pair_bias[:, t * P:(t + 1) * P, :].rearrange("h p k -> p h k")
                                 ).then_inc(weights_in, 16)

                def step(i, s):
                    wait_unit(sp, projected, i - AHEAD)
                    sp.dma_start(xT[s][:], normed[i]).then_inc(xT_loaded[s], 16)
                    wait_unit(sp, x_bo_ready, i - AHEAD)
                    sp.dma_start(x_res[s][:], x_rows[i]).then_inc(res_loaded[s], 16)

                each_unit(sp, ROWS, AHEAD, step)

            @block.tensor
            def _(pe):
                pe.wait_ge(w_ready, 2)
                pe.wait_ge(ident_ready, 4)

                def project(i, s):
                    wait_dma(pe, xT_loaded, i, s, AHEAD)
                    wait_unit(pe, even_ready, i - 2, per=2)
                    wait_unit(pe, qk_ready, i - 1)
                    nc.tensor.matmul(bank_a[:, 0, :], w["q"][:], xT[s][:], start=True, stop=True)
                    nc.tensor.matmul(bank_a[:, 1, :], w["k"][:], xT[s][:], start=True, stop=True)
                    wait_unit(pe, gv_ready, i - 1)
                    nc.tensor.matmul(bank_b[:, 0, :], w["g"][:], xT[s][:], start=True, stop=True)
                    for t in range(2):
                        last = nc.tensor.matmul(bank_b[:, 1, t * P:(t + 1) * P], xT[s][:, t * P:(t + 1) * P], w["v"][:],
                                                start=True, stop=True)
                    last.then_inc(projected, 1)

                def score(i, s):
                    wait_unit(pe, qk_ready, i)
                    for h in range(HEADS):
                        rows = slice(h * HEAD_DIM, (h + 1) * HEAD_DIM)
                        wait_unit(pe, biased, i - 1, per=HEADS, part=h + 1)
                        for t in range(2):
                            last = nc.tensor.matmul(scores[h][:, t, :], qk[s % 2][rows, 0, t * P:(t + 1) * P],
                                                    qk[s % 2][rows, 1, :], start=True, stop=True)
                        last.then_inc(scored, 1)

                project(0, 0)
                score(0, 0)
                project(1, 1)

                def step(i, s):
                    if exists(i + 1, ROWS):
                        score(i + 1, (s + 1) % AHEAD)
                    for h in range(HEADS):
                        wait_unit(pe, exp_ready, i, per=HEADS, part=h + 1)
                        if h == 0:
                            wait_unit(pe, qk_ready, i + 1 if exists(i + 1, ROWS) else i)
                        elif h == 2:
                            wait_unit(pe, even_ready, i, per=2, part=1)
                        elif h == 1:
                            wait_unit(pe, gate_inv_ready, i - 1)
                        else:
                            wait_unit(pe, odd_ready, i, per=2, part=1)
                        bank = bank_c if h % 2 else bank_a
                        for k in range(2):
                            for t in range(2):
                                last = nc.tensor.transpose(bank[:, k, t * P:(t + 1) * P],
                                                           probs[s % 2][:, h, t, k * P:(k + 1) * P], ident[:])
                        last.then_inc(turned, 1)
                    if exists(i + 2, ROWS):
                        project(i + 2, (s + 2) % AHEAD)
                    wait_unit(pe, inv_ready, i)
                    wait_unit(pe, odd_ready, i, per=2)
                    for t in range(2):
                        for h in range(HEADS):
                            n = h * 2 + t
                            last = nc.tensor.matmul(bank_c[h * HEAD_DIM:(h + 1) * HEAD_DIM, 0, t * P:(t + 1) * P],
                                                    inv[s % 2][:, n:n + 1].to_broadcast([P, HEAD_DIM]), half_ident[:],
                                                    start=True, stop=True)
                    last.then_inc(inv_turned, 1)
                    wait_unit(pe, even_ready, i, per=2)
                    wait_unit(pe, gv_ready, i)
                    wait_unit(pe, x1_ready, i - 1)
                    for k in range(2):
                        for h in range(HEADS):
                            rows = slice(h * HEAD_DIM, (h + 1) * HEAD_DIM)
                            last = nc.tensor.matmul(bank_d[rows, 0, :], v[s][:, k, rows], probsT[:, h, k, :],
                                                    start=(k == 0), stop=(k == 1))
                    last.then_inc(valued, 1)
                    wait_unit(pe, valuesT_ready, i)
                    for t in range(2):
                        last = nc.tensor.matmul(bank_d[:, 1, t * P:(t + 1) * P], valuesT[s % 2][:, t * P:(t + 1) * P],
                                                w["o"][:], start=True, stop=True)
                    last.then_inc(out_ready, 1)

                each_unit(pe, ROWS, AHEAD, step)

            @block.vector
            def _(dve):
                dve.wait_ge(weights_in, loads)
                nc.vector.tensor_scalar(half_bg[:], bg_col[:], 0.5, None, ALU.mult).then_inc(w_ready, 1)
                nc.vector.tensor_scalar(w["q"][:], w["q_raw"][:], scale, None, ALU.mult).then_inc(w_ready, 1)

                def add_bias(i, s):
                    for h in range(HEADS):
                        if h == 0:
                            wait_unit(dve, turned, i - 2, per=HEADS)
                        wait_unit(dve, scored, i, per=HEADS, part=h + 1)
                        nc.vector.tensor_copy(wait_tick[:, h:h + 1], bg_col[:])
                        for t in range(2):
                            n = h * 2 + t
                            last = nc.vector.tensor_tensor_reduce(
                                out=probs[s % 2][:, h, t, :], in0=scores[h][:, t, :], in1=bias[:, h, t, :], scale=1.0,
                                scalar=LOWEST, op0=ALU.add, op1=ALU.max, accum_out=top[s % 2][:, n:n + 1])
                        last.then_inc(biased, 1)
                    wait_unit(dve, biased, i, per=HEADS)
                    nc.vector.tensor_scalar(neg_top[s % 2][:], top[s % 2][:], -1.0, None, ALU.mult).then_inc(neg_ready, 1)

                add_bias(0, 0)

                def step(i, s):
                    if exists(i + 1, ROWS):
                        add_bias(i + 1, (s + 1) % AHEAD)
                    for part in range(2):
                        wait_unit(dve, turned, i, per=HEADS, part=2 * part + 1)
                        if part == 0:
                            wait_unit(dve, valued, i - 1)
                        nc.vector.tensor_copy(probsT[:, 2 * part], bank_a[:]).then_inc(even_ready, 1)
                    wait_unit(dve, exp_ready, i, per=HEADS)
                    nc.vector.reciprocal(inv[s % 2][:], total[s % 2][:]).then_inc(inv_ready, 1)
                    wait_unit(dve, inv_turned, i)
                    wait_unit(dve, gv_ready, i)
                    nc.vector.scalar_tensor_tensor(gate_inv[:], gate[s][:], 1.0, bank_c[:, 0, :], ALU.add, ALU.mult
                                                   ).then_inc(gate_inv_ready, 1)
                    wait_unit(dve, valued, i)
                    wait_unit(dve, gate_inv_ready, i)
                    nc.vector.tensor_tensor(valuesT[s % 2][:], bank_d[:, 0, :], gate_inv[:], ALU.mult
                                            ).then_inc(valuesT_ready, 1)
                    wait_unit(dve, out_ready, i)
                    wait_unit(dve, x_bo_ready, i)
                    wait_dma(dve, x1_stored, i - 2, s % 2)
                    nc.vector.tensor_tensor(x1_out[s % 2][:].rearrange("p t c -> p (t c)"), bank_d[:, 1, :],
                                            x_bo[s % 2][:].rearrange("p t c -> p (t c)"), ALU.add).then_inc(x1_ready, 1)

                each_unit(dve, ROWS, AHEAD, step)

            @block.gpsimd
            def _(pool):
                make_identity(nc, ident, ident_ready)
                pool.wait_ge(ident_ready, 2)
                nc.gpsimd.memset(half_ident[:], 0.0).then_inc(ident_ready, 1)
                pool.wait_ge(ident_ready, 3)
                nc.gpsimd.affine_select(out=half_ident[:], in_=half_ident[:], compare_op=ALU.not_equal, fill=0.5, base=0,
                                        pattern=[[-1, P]], channel_multiplier=1).then_inc(ident_ready, 1)
                pool.wait_ge(weights_in, loads)

                def step(i, s):
                    wait_dma(pool, res_loaded, i, s, AHEAD)
                    wait_unit(pool, x1_ready, i - 2)
                    nc.gpsimd.tensor_tensor(x_bo[s % 2][:], x_res[s][:], bo_all[:].unsqueeze(1).to_broadcast([P, 2, C]),
                                            ALU.add).then_inc(x_bo_ready, 1)

                each_unit(pool, ROWS, AHEAD, step)

            @block.scalar
            def _(act):
                act.wait_ge(w_ready, 2)

                def take_projections(i, s):
                    wait_unit(act, projected, i)
                    wait_unit(act, scored, i - 2, per=HEADS)
                    nc.scalar.copy(qk[s % 2][:], bank_a[:]).then_inc(qk_ready, 1)
                    nc.scalar.activation(gate[s][:], bank_b[:, 0, :], ACT.Tanh, scale=0.5, bias=half_bg[:, 0:1])
                    nc.scalar.copy(v[s][:].rearrange("p t c -> p (t c)"), bank_b[:, 1, :]).then_inc(gv_ready, 1)

                take_projections(0, 0)
                take_projections(1, 1)

                def step(i, s):
                    wait_unit(act, neg_ready, i)
                    wait_unit(act, inv_ready, i - 2)
                    for h in range(HEADS):
                        for t in range(2):
                            n = h * 2 + t
                            last = nc.scalar.activation(probs[s % 2][:, h, t, :], probs[s % 2][:, h, t, :], ACT.Exp,
                                                        bias=neg_top[s % 2][:, n:n + 1],
                                                        accum_out=total[s % 2][:, n:n + 1])
                        last.then_inc(exp_ready, 1)
                    for part in range(2):
                        wait_unit(act, turned, i, per=HEADS, part=2 * part + 2)
                        if part == 0:
                            wait_unit(act, valued, i - 1)
                        nc.scalar.copy(probsT[:, 2 * part + 1], bank_c[:]).then_inc(odd_ready, 1)
                    if exists(i + 2, ROWS):
                        take_projections(i + 2, (s + 2) % AHEAD)
                    if exists(i - 1, ROWS):
                        store(i - 1, (s - 1) % AHEAD)

                def store(i, s):
                    wait_unit(act, x1_ready, i)
                    act.dma_start(x1_rows[i], x1_out[s % 2][:]).then_inc(x1_stored[s % 2], 16)

                each_unit(act, ROWS, AHEAD, step)
                store(ROWS - 1, AHEAD - 1)
                for s in range(2):
                    wait_dma(act, x1_stored, ROWS - 2 + s, s)

        mem.clear()



CHUNK = 64
HALVES = 2
HALF = TOKENS // HALVES
CHUNKS = HALF // CHUNK
GROUPS = 2
LANES = CHUNKS // GROUPS
WARM = 16
TOLERANCE = 2.0 ** -21


def recurrence(nc, wx, wx_stats, V, gamma, beta, y_out):
    with ExitStack() as stack:
        mem = Memory(nc, stack, "rec")
        steps = mem.sbuf("steps", [C, HALF])
        lanes = steps[:].rearrange("c (g n k) -> c g n k", g=GROUPS, k=CHUNK)
        first = mem.sbuf("first", [C, CHUNKS + 1])
        warm = [[mem.sbuf(f"warm{g}{p}", [C, LANES]) for p in range(2)] for g in range(GROUPS)]
        z = [mem.sbuf(f"z{g}", [C, LANES]) for g in range(GROUPS)]
        vT, v_raw, ident = mem.sbuf("vT", [C, C]), mem.sbuf("v_raw", [C, C]), mem.sbuf("ident", [P, P])
        g_col, b_col, ones = mem.sbuf("g_col", [C, 1]), mem.sbuf("b_col", [C, 1]), mem.sbuf("ones", [C, 1])
        scale, shift, tmp = mem.sbuf("scale", [C, 1]), mem.sbuf("shift", [C, 1]), mem.sbuf("tmp", [C, 4])
        gap = mem.sbuf("gap", [C, CHUNKS])
        near = mem.sbuf("near", [C, 1])
        redo = mem.sbuf("redo", [1, 1], I32)
        y_last = mem.sbuf("y_last", [C, 1])
        product = [mem.psum(f"product{g}", [C, LANES]) for g in range(GROUPS)]
        turned = mem.psum("turned", [C, C])
        count = mem.psum("count", [1, 1])
        single = mem.psum("single", [C, 1])

        weights_in, ident_ready, v_turned, ready = (mem.sem(n) for n in ("weights_in", "ident", "v_turned", "ready"))
        multiplied = [mem.sem(f"multiplied{g}") for g in range(GROUPS)]
        summed = [mem.sem(f"summed{g}") for g in range(GROUPS)]
        stepped = [mem.sem(f"stepped{g}") for g in range(GROUPS)]
        halves = [{n: mem.sem(f"{n}{h}") for n in
                   ("loaded", "chain", "near", "counted", "redo_ready", "reloaded", "ready_again", "slow_product",
                    "slow_step", "stored", "kept")} for h in range(HALVES)]
        setup = 6
        per_half = WARM + CHUNK
        units_half = UNITS // HALVES

        with nc.Block() as block:
            @block.sync
            def _(sp):
                sp.dma_start(v_raw[:], V).then_inc(weights_in, 16)
                sp.dma_start(g_col[:], column(gamma)).then_inc(weights_in, 16)
                sp.dma_start(b_col[:], column(beta)).then_inc(weights_in, 16)
                for h, sems in enumerate(halves):
                    def load(done):
                        for u in range(units_half):
                            sp.dma_start(steps[:, u * UNIT:(u + 1) * UNIT], wx[h * units_half + u]).then_inc(done, 16)

                    if h:
                        sp.wait_ge(halves[h - 1]["kept"], 1)
                    load(sems["loaded"])
                    sp.wait_ge(sems["redo_ready"], 1)
                    again = sp.value_load(redo[0:1, 0:1], min_val=0, max_val=1)
                    with sp.If(again == 1):
                        load(sems["reloaded"])
                        sp.wait_ge(sems["slow_step"], HALF)
                    for u in range(units_half):
                        sp.dma_start(y_out[h * units_half + u], steps[:, u * UNIT:(u + 1) * UNIT]).then_inc(sems["stored"], 16)
                    sp.wait_ge(sems["stored"], 16 * units_half)

            @block.gpsimd
            def _(pool):
                nc.gpsimd.memset(ones[:], 1.0).then_inc(ident_ready, 1)
                nc.gpsimd.memset(ident[:], 0.0).then_inc(ident_ready, 1)
                pool.wait_ge(ident_ready, 2)
                nc.gpsimd.affine_select(out=ident[:], in_=ident[:], compare_op=ALU.not_equal, fill=1.0, base=0,
                                        pattern=[[-1, P]], channel_multiplier=1).then_inc(ident_ready, 1)
                pool.wait_ge(weights_in, 48)
                g = nc.gpsimd
                g.memset(tmp[:, 3:4], -0.5).then_inc(ready, 1)
                g.tensor_scalar(tmp[:, 0:1], wx_stats[:, 1:2], 1.0, EPS_BN, ALU.mult, ALU.add).then_inc(ready, 1)
                pool.wait_ge(ready, 2)
                g.tensor_tensor(tmp[:, 1:2], tmp[:, 0:1], tmp[:, 3:4], ALU.pow).then_inc(ready, 1)
                pool.wait_ge(ready, 3)
                g.tensor_tensor(scale[:], g_col[:], tmp[:, 1:2], ALU.mult).then_inc(ready, 1)
                pool.wait_ge(ready, 4)
                g.tensor_tensor(tmp[:, 2:3], scale[:], wx_stats[:, 0:1], ALU.mult).then_inc(ready, 1)
                pool.wait_ge(ready, 5)
                g.tensor_tensor(shift[:], b_col[:], tmp[:, 2:3], ALU.subtract).then_inc(ready, 1)

            @block.tensor
            def _(pe):
                pe.wait_ge(weights_in, 48)
                pe.wait_ge(ident_ready, 3)
                nc.tensor.transpose(turned[:], v_raw[:], ident[:]).then_inc(v_turned, 1)
                pe.wait_ge(v_turned, 2)

                def multiply(g, rhs, n):
                    pe.wait_ge(stepped[g], n)
                    nc.tensor.matmul(product[g][:], vT[:], rhs, start=True, stop=True).then_inc(multiplied[g], 1)

                for h, sems in enumerate(halves):
                    base = h * (per_half + 1)
                    for g in range(GROUPS):
                        multiply(g, warm[g][1][:], base + 1)
                    with pe.Fori(1, WARM - 1, 2) as k:
                        for odd in range(2):
                            for g in range(GROUPS):
                                multiply(g, warm[g][odd][:], k + (base + 1 + odd))
                    for g in range(GROUPS):
                        multiply(g, warm[g][0][:], base + WARM)
                    pe.wait_ge(stepped[0], base + WARM + 1)
                    for g in range(GROUPS):
                        multiply(g, first[:, g * LANES:(g + 1) * LANES], base + WARM + 1)
                    with pe.Fori(1, CHUNK) as k:
                        for g in range(GROUPS):
                            multiply(g, lanes[:, g, :, bass.ds(k - 1, 1)].rearrange("c n k -> c (n k)"), k + (base + WARM + 1))
                    pe.wait_ge(sems["near"], 1)
                    nc.tensor.matmul(count[:], near[:], ones[:], start=True, stop=True).then_inc(sems["counted"], 1)
                    pe.wait_ge(sems["redo_ready"], 1)
                    again = pe.value_load(redo[0:1, 0:1], min_val=0, max_val=1)
                    with pe.If(again == 1):
                        pe.wait_ge(sems["ready_again"], 1)
                        nc.tensor.matmul(single[:], vT[:], first[:, 0:1], start=True, stop=True).then_inc(sems["slow_product"], 1)
                        with pe.Fori(1, HALF) as t:
                            pe.wait_ge(sems["slow_step"], t)
                            nc.tensor.matmul(single[:], vT[:], steps[:, bass.ds(t - 1, 1)], start=True, stop=True
                                             ).then_inc(sems["slow_product"], 1)

            @block.vector
            def _(dve):
                dve.wait_ge(v_turned, 1)
                nc.vector.tensor_copy(vT[:], turned[:]).then_inc(v_turned, 1)
                dve.wait_ge(ready, setup)

                def add(g, part, n):
                    dve.wait_ge(multiplied[g], n)
                    nc.vector.scalar_tensor_tensor(z[g][:], part, scale[:, 0:1], product[g][:], ALU.mult, ALU.add
                                                   ).then_inc(summed[g], 1)

                for h, sems in enumerate(halves):
                    base = h * per_half
                    if h:
                        dve.wait_ge(halves[h - 1]["kept"], 1)
                    else:
                        nc.vector.memset(y_last[:], 0.0).then_inc(sems["chain"], 1)
                        dve.wait_ge(sems["chain"], 1)
                    chain = 1 if h == 0 else 0
                    nc.vector.tensor_copy(first[:, 0:1], y_last[:]).then_inc(sems["chain"], 1)
                    for g in range(GROUPS):
                        nc.vector.memset(warm[g][1][:], 0.0).then_inc(stepped[g], 1)
                    dve.wait_ge(sems["loaded"], 16 * units_half)
                    dve.wait_ge(sems["chain"], chain + 1)
                    with dve.Fori(0, WARM) as k:
                        for g in range(GROUPS):
                            add(g, lanes[:, g, :, bass.ds(k + (CHUNK - WARM), 1)].rearrange("c n k -> c (n k)"), k + (base + 1))
                    with dve.Fori(0, CHUNK) as k:
                        for g in range(GROUPS):
                            add(g, lanes[:, g, :, bass.ds(k, 1)].rearrange("c n k -> c (n k)"), k + (base + WARM + 1))
                    for g in range(GROUPS):
                        dve.wait_ge(stepped[g], (h + 1) * (per_half + 1))
                    link = sems["chain"]
                    ends = steps[:].rearrange("c (n k) -> c n k", k=CHUNK)[:, :, CHUNK - 1]
                    nc.vector.tensor_tensor(gap[:], ends, first[:, 1:CHUNKS + 1], ALU.subtract).then_inc(link, 1)
                    dve.wait_ge(link, chain + 2)
                    nc.vector.tensor_tensor(gap[:], gap[:], gap[:], ALU.mult).then_inc(link, 1)
                    dve.wait_ge(link, chain + 3)
                    nc.vector.tensor_scalar(gap[:], gap[:], TOLERANCE ** 2, None, ALU.is_le).then_inc(link, 1)
                    dve.wait_ge(link, chain + 4)
                    nc.vector.tensor_reduce(out=near[:], in_=gap[:], axis=AX.X, op=ALU.min).then_inc(sems["near"], 1)
                    dve.wait_ge(sems["counted"], 1)
                    nc.vector.tensor_scalar(redo[:], count[:], float(C) - 0.5, None, ALU.is_lt).then_inc(sems["redo_ready"], 1)
                    dve.wait_ge(sems["redo_ready"], 1)
                    again = dve.value_load(redo[0:1, 0:1], min_val=0, max_val=1)
                    with dve.If(again == 1):
                        dve.wait_ge(sems["reloaded"], 16 * units_half)
                        with dve.Fori(0, units_half) as u:
                            nc.vector.tensor_scalar(steps[:, bass.ds(u * UNIT, UNIT)], steps[:, bass.ds(u * UNIT, UNIT)],
                                                    scale[:, 0:1], shift[:, 0:1], ALU.mult, ALU.add)
                        nc.vector.tensor_copy(near[:], ones[:]).then_inc(sems["ready_again"], 1)
                        dve.wait_ge(sems["slow_step"], HALF)
                    nc.vector.tensor_copy(y_last[:], steps[:, HALF - 1:HALF]).then_inc(sems["kept"], 1)

            @block.scalar
            def _(act):
                act.wait_ge(ready, setup)

                def state(g, out, n):
                    act.wait_ge(summed[g], n)
                    nc.scalar.activation(out, z[g][:], ACT.Sigmoid, bias=shift[:, 0:1]).then_inc(stepped[g], 1)

                for h, sems in enumerate(halves):
                    base = h * per_half
                    with act.Fori(0, WARM - 2, 2) as k:
                        for odd in range(2):
                            for g in range(GROUPS):
                                state(g, warm[g][odd][:], k + (base + 1 + odd))
                    for g in range(GROUPS):
                        state(g, warm[g][0][:], base + WARM - 1)
                    for g in range(GROUPS):
                        state(g, first[:, g * LANES + 1:(g + 1) * LANES + 1], base + WARM)
                    with act.Fori(0, CHUNK) as k:
                        for g in range(GROUPS):
                            state(g, lanes[:, g, :, bass.ds(k, 1)].rearrange("c n k -> c (n k)"), k + (base + WARM + 1))
                    act.wait_ge(sems["redo_ready"], 1)
                    again = act.value_load(redo[0:1, 0:1], min_val=0, max_val=1)
                    with act.If(again == 1):
                        act.wait_ge(sems["ready_again"], 1)
                        with act.Fori(0, HALF) as t:
                            act.wait_ge(sems["slow_product"], t + 1)
                            nc.scalar.activation(steps[:, bass.ds(t, 1)], single[:], ACT.Sigmoid,
                                                 bias=steps[:, bass.ds(t, 1)]).then_inc(sems["slow_step"], 1)

        mem.clear()


def gates(nc, x1, y, norm_g, norm_b, weights, biases, x2, left, right, out_gate):
    with ExitStack() as stack:
        mem = Memory(nc, stack, "gates")
        norm = RowNorm(mem, 1 + EPS_LN, EPS_C * EPS_LN)
        x_in = [mem.sbuf(f"x{s}", [P, TILES, C]) for s in range(2)]
        y_in = [mem.sbuf(f"y{s}", [C, UNIT]) for s in range(2)]
        x2_sb = [mem.sbuf(f"x2{s}", [P, TILES, C]) for s in range(AHEAD)]
        centred = [mem.sbuf(f"centred{s}", [P, TILES, C]) for s in range(2)]
        xT = [mem.sbuf(f"xT{s}", [C, UNIT]) for s in range(2)]
        sides = [[mem.sbuf(f"side{n}{s}", [C, UNIT]) for s in range(2)] for n in range(2)]
        gate = [mem.sbuf(f"gate{s}", [C, BANK]) for s in range(2)]
        og = [mem.sbuf(f"og{s}", [C, UNIT]) for s in range(2)]
        w = [mem.sbuf(f"w{n}", [C, C]) for n in range(5)]
        b = [mem.sbuf(f"b{n}", [C, 1]) for n in range(5)]
        g_col, b_col, ident = mem.sbuf("g_col", [C, 1]), mem.sbuf("b_col", [C, 1]), mem.sbuf("ident", [P, P])
        y_turned = mem.psum("y_turned", [P, TILES, C])
        turned = mem.psum("turned", [C, UNIT])
        gate_bank = [mem.psum(f"gate_bank{n}", [C, BANK]) for n in range(2)]
        side_bank = [mem.psum(f"side_bank{n}", [C, BANK]) for n in range(2)]

        weights_in, ident_ready = mem.sem("weights_in"), mem.sem("ident")
        x_loaded, y_loaded = mem.sems("x_loaded"), mem.sems("y_loaded")
        x2_stored, left_stored, right_stored, og_stored = mem.sems("x2_stored", AHEAD), mem.sems("left_stored"), mem.sems("right_stored"), mem.sems("og_stored")
        (y_turned_ready, x2_ready, stats_ready, rstd_ready, centred_ready, turned_ready, xT_ready, gate_product,
         side_product, gate_ready, side_ready) = (mem.sem(n) for n in (
             "y_turned_ready", "x2_ready", "stats", "rstd", "centred_ready", "turned_ready", "xT_ready", "gate_product",
             "side_product", "gate_ready", "side_ready"))
        loads = 16 * 12
        GATES_A_UNIT, SIDES_A_UNIT = 6, 4
        x_units = x1.rearrange("(u t p) c -> u p t c", t=TILES, p=P)
        x2_units = x2.rearrange("(u t p) c -> u p t c", t=TILES, p=P)

        with nc.Block() as block:
            @block.sync
            def _(sp):
                for n in range(5):
                    sp.dma_start(w[n][:], weights[n]).then_inc(weights_in, 16)
                    sp.dma_start(b[n][:], column(biases[n])).then_inc(weights_in, 16)
                sp.dma_start(g_col[:], column(norm_g)).then_inc(weights_in, 16)
                sp.dma_start(b_col[:], column(norm_b)).then_inc(weights_in, 16)

                def step(u, s):
                    wait_unit(sp, x2_ready, u - 2)
                    sp.dma_start(x_in[s][:], x_units[u]).then_inc(x_loaded[s], 16)
                    sp.dma_start(y_in[s][:], y[u]).then_inc(y_loaded[s], 16)

                each_unit(sp, UNITS, 2, step)

            @block.tensor
            def _(pe):
                pe.wait_ge(ident_ready, 2)
                pe.wait_ge(weights_in, loads)

                def turn_y(u, s):
                    wait_dma(pe, y_loaded, u, s % 2)
                    wait_unit(pe, x2_ready, u - 1)
                    for t in range(TILES):
                        last = nc.tensor.transpose(y_turned[:, t, :], y_in[s % 2][:, t * P:(t + 1) * P], ident[:])
                    last.then_inc(y_turned_ready, 1)

                def project(u, s):
                    wait_unit(pe, xT_ready, u)
                    for half in range(2):
                        rhs = xT[s % 2][:, half * BANK:(half + 1) * BANK]
                        for n in range(5):
                            if n in (1, 3):
                                k = 2 * half + (n == 3)
                                wait_count(pe, side_ready, u * SIDES_A_UNIT + (k - 1))
                                nc.tensor.matmul(side_bank[k % 2][:], w[n][:], rhs, start=True, stop=True
                                                 ).then_inc(side_product, 1)
                            else:
                                k = 3 * half + n // 2
                                wait_count(pe, gate_ready, u * GATES_A_UNIT + (k - 1))
                                nc.tensor.matmul(gate_bank[k % 2][:], w[n][:], rhs, start=True, stop=True
                                                 ).then_inc(gate_product, 1)

                turn_y(0, 0)
                turn_y(1, 1)

                def step(u, s):
                    wait_unit(pe, centred_ready, u)
                    wait_unit(pe, xT_ready, u - 1)
                    for t in range(TILES):
                        last = nc.tensor.transpose(turned[:, t * P:(t + 1) * P], centred[s % 2][:, t, :], ident[:])
                    last.then_inc(turned_ready, 1)
                    if exists(u - 1, UNITS):
                        project(u - 1, s - 1)
                    if exists(u + 2, UNITS):
                        turn_y(u + 2, s)

                each_unit(pe, UNITS, AHEAD, step)
                project(UNITS - 1, UNITS - 1)

            @block.vector
            def _(dve):
                def add_y(u, s):
                    wait_dma(dve, x_loaded, u, s % 2)
                    wait_unit(dve, y_turned_ready, u)
                    wait_unit(dve, centred_ready, u - AHEAD)
                    wait_dma(dve, x2_stored, u - AHEAD, s % AHEAD, AHEAD)
                    nc.vector.tensor_tensor(x2_sb[s % AHEAD][:].rearrange("p t c -> p (t c)"),
                                            y_turned[:].rearrange("p t c -> p (t c)"),
                                            x_in[s % 2][:].rearrange("p t c -> p (t c)"), ALU.add).then_inc(x2_ready, 1)
                    wait_unit(dve, x2_ready, u)
                    tile_stats(nc, norm.stats[s % 2], x2_sb[s % AHEAD], stats_ready)

                def multiply(u, s):
                    for half in range(2):
                        for n in range(2):
                            k = 2 * half + n
                            if half == 0:
                                wait_dma(dve, (left_stored, right_stored)[n], u - 2, s % 2)
                            wait_count(dve, side_product, u * SIDES_A_UNIT + (k + 1))
                            wait_count(dve, gate_ready, u * GATES_A_UNIT + (3 * half + n + 1))
                            nc.vector.scalar_tensor_tensor(sides[n][s % 2][:, half * BANK:(half + 1) * BANK],
                                                           side_bank[k % 2][:], b[2 * n + 1][:, 0:1], gate[n][:],
                                                           ALU.add, ALU.mult).then_inc(side_ready, 1)

                dve.wait_ge(weights_in, loads)
                add_y(0, 0)

                def step(u, s):
                    if exists(u + 1, UNITS):
                        add_y(u + 1, s + 1)
                    wait_unit(dve, rstd_ready, u)
                    wait_unit(dve, turned_ready, u - 2)
                    norm.apply(nc, s % 2, centred[s % 2], x2_sb[s % AHEAD], centred_ready)
                    if exists(u - 1, UNITS):
                        multiply(u - 1, s + 1)

                each_unit(dve, UNITS, AHEAD, step)
                multiply(UNITS - 1, UNITS - 1)

            @block.gpsimd
            def _(pool):
                make_identity(nc, ident, ident_ready)
                norm.prepare(nc)

                def step(u, s):
                    wait_unit(pool, stats_ready, u)
                    wait_unit(pool, centred_ready, u - 2)
                    norm.rstd_of(nc, u, s, rstd_ready)

                each_unit(pool, UNITS, 2, step)

            @block.scalar
            def _(act):
                act.wait_ge(weights_in, loads)

                def take_gates(u, s):
                    for half in range(2):
                        for n in range(3):
                            k = 3 * half + n
                            wait_count(act, gate_product, u * GATES_A_UNIT + (k + 1))
                            if n < 2:
                                wait_count(act, side_ready, u * SIDES_A_UNIT + (2 * half + n - 1))
                                out = gate[n][:]
                            else:
                                if half == 0:
                                    wait_dma(act, og_stored, u - 2, s % 2)
                                out = og[s % 2][:, half * BANK:(half + 1) * BANK]
                            nc.scalar.activation(out, gate_bank[k % 2][:], ACT.Sigmoid, bias=b[2 * n][:, 0:1]
                                                 ).then_inc(gate_ready, 1)

                def store(u, s):
                    wait_unit(act, side_ready, u, per=SIDES_A_UNIT)
                    wait_unit(act, gate_ready, u, per=GATES_A_UNIT)
                    cols = bass.ds(u * UNIT, UNIT)
                    act.dma_start(left[:, cols], sides[0][s % 2][:]).then_inc(left_stored[s % 2], 16)
                    act.dma_start(right[:, cols], sides[1][s % 2][:]).then_inc(right_stored[s % 2], 16)
                    act.dma_start(out_gate[u], og[s % 2][:]).then_inc(og_stored[s % 2], 16)

                def step(u, s):
                    wait_unit(act, x2_ready, u)
                    act.dma_start(x2_units[u], x2_sb[s % AHEAD][:]).then_inc(x2_stored[s % AHEAD], 16)
                    wait_unit(act, turned_ready, u)
                    wait_unit(act, gate_product, u - 2, per=GATES_A_UNIT)
                    wait_unit(act, side_product, u - 2, per=SIDES_A_UNIT)
                    for half in range(2):
                        cols = slice(half * BANK, (half + 1) * BANK)
                        last = nc.scalar.activation(xT[s % 2][:, cols], turned[:, cols], ACT.Identity,
                                                    scale=g_col[:, 0:1], bias=b_col[:, 0:1])
                    last.then_inc(xT_ready, 1)
                    if exists(u - 1, UNITS):
                        take_gates(u - 1, s + 1)
                        store(u - 1, s + 1)

                each_unit(act, UNITS, AHEAD, step)
                take_gates(UNITS - 1, UNITS - 1)
                store(UNITS - 1, UNITS - 1)
                for s in range(2):
                    for sems in (left_stored, right_stored, og_stored):
                        wait_dma(act, sems, UNITS - 2 + s, s)
                for s in range(AHEAD):
                    wait_dma(act, x2_stored, UNITS - AHEAD + s, s, AHEAD)

        mem.clear()


def triangle(nc, left, right, out):
    with ExitStack() as stack:
        mem = Memory(nc, stack, "tri")
        l = [mem.sbuf(f"l{s}", [P, 2, COLS]) for s in range(AHEAD)]
        r = [mem.sbuf(f"r{s}", [P, 2, COLS]) for s in range(AHEAD)]
        o = [mem.sbuf(f"o{s}", [P, 2, COLS]) for s in range(AHEAD)]
        product = [mem.psum(f"product{s}", [P, 2, COLS]) for s in range(AHEAD)]
        l_loaded, r_loaded, stored = mem.sems("l_loaded", AHEAD), mem.sems("r_loaded", AHEAD), mem.sems("stored", AHEAD)
        multiplied, o_ready = mem.sem("multiplied"), mem.sem("o_ready")

        def channel(t, d):
            return t[bass.ds(d, 1), 0:TOKENS].rearrange("a (k p j) -> p (a k) j", k=2, p=P)

        with nc.Block() as block:
            @block.sync
            def _(sp):
                def step(d, s):
                    wait_unit(sp, multiplied, d - AHEAD)
                    sp.dma_start(l[s][:], channel(left, d)).then_inc(l_loaded[s], 16)
                    sp.dma_start(r[s][:], channel(right, d)).then_inc(r_loaded[s], 16)

                each_unit(sp, C, AHEAD, step)

            @block.tensor
            def _(pe):
                def step(d, s):
                    wait_dma(pe, l_loaded, d, s, AHEAD)
                    wait_dma(pe, r_loaded, d, s, AHEAD)
                    wait_unit(pe, o_ready, d - AHEAD)
                    for i in range(2):
                        for k in range(2):
                            last = nc.tensor.matmul(product[s][:, i, :], r[s][:, k, i * P:(i + 1) * P], l[s][:, k, :],
                                                    start=(k == 0), stop=(k == 1))
                    last.then_inc(multiplied, 1)

                each_unit(pe, C, AHEAD, step)

            @block.vector
            def _(dve):
                def step(d, s):
                    wait_unit(dve, multiplied, d)
                    wait_dma(dve, stored, d - AHEAD, s, AHEAD)
                    nc.vector.tensor_copy(o[s][:], product[s][:]).then_inc(o_ready, 1)

                each_unit(dve, C, AHEAD, step)

            @block.scalar
            def _(act):
                def step(d, s):
                    wait_unit(act, o_ready, d)
                    act.dma_start(channel(out, d), o[s][:]).then_inc(stored[s], 16)

                each_unit(act, C, AHEAD, step)
                for s in range(AHEAD):
                    wait_dma(act, stored, C - AHEAD + s, s, AHEAD)

        mem.clear()


def triangle_out(nc, tri, out_gate, x2, norm_g, norm_b, w_out, b_out, x3):
    with ExitStack() as stack:
        mem = Memory(nc, stack, "out")
        norm = RowNorm(mem, 1.0, EPS_LN)
        tri_in = [mem.sbuf(f"tri{s}", [C, UNIT]) for s in range(2)]
        og = [mem.sbuf(f"og{s}", [C, UNIT]) for s in range(AHEAD)]
        x_in = [mem.sbuf(f"x{s}", [P, TILES, C]) for s in range(AHEAD)]
        centred = [mem.sbuf(f"centred{s}", [P, TILES, C]) for s in range(2)]
        normed = [mem.sbuf(f"normed{s}", [C, UNIT]) for s in range(2)]
        gated = [mem.sbuf(f"gated{s}", [C, UNIT]) for s in range(2)]
        x_b = [mem.sbuf(f"x_b{s}", [P, TILES, C]) for s in range(2)]
        x3_sb = [mem.sbuf(f"x3{s}", [P, TILES, C]) for s in range(2)]
        w, b_all, ident = mem.sbuf("w", [C, C]), mem.sbuf("b_all", [P, C]), mem.sbuf("ident", [P, P])
        g_col, b_col = mem.sbuf("g_col", [C, 1]), mem.sbuf("b_col", [C, 1])
        tokens = [mem.psum(f"tokens{s}", [P, TILES, C]) for s in range(2)]
        turned = mem.psum("turned", [C, UNIT])
        product = mem.psum("product", [P, TILES, C])

        weights_in, ident_ready = mem.sem("weights_in"), mem.sem("ident")
        tri_loaded, og_loaded, x_loaded = mem.sems("tri_loaded"), mem.sems("og_loaded", AHEAD), mem.sems("x_loaded", AHEAD)
        stored = mem.sems("stored")
        (tokens_ready, stats_ready, rstd_ready, centred_ready, turned_ready, normed_ready, gated_ready, product_ready,
         x_b_ready, x3_ready) = (mem.sem(n) for n in ("tokens_ready", "stats", "rstd", "centred_ready", "turned_ready",
                                                      "normed_ready", "gated_ready", "product_ready", "x_b_ready", "x3_ready"))
        loads = 16 * 4
        x_units = x2.rearrange("(u t p) c -> u p t c", t=TILES, p=P)
        x3_units = x3.rearrange("(u t p) c -> u p t c", t=TILES, p=P)

        with nc.Block() as block:
            @block.sync
            def _(sp):
                sp.dma_start(w[:], w_out).then_inc(weights_in, 16)
                sp.dma_start(b_all[:], row_to_all(b_out)).then_inc(weights_in, 16)
                sp.dma_start(g_col[:], column(norm_g)).then_inc(weights_in, 16)
                sp.dma_start(b_col[:], column(norm_b)).then_inc(weights_in, 16)

                def step(u, s):
                    wait_unit(sp, tokens_ready, u - 2)
                    sp.dma_start(tri_in[s % 2][:], tri[:, bass.ds(u * UNIT, UNIT)]).then_inc(tri_loaded[s % 2], 16)
                    wait_unit(sp, x_b_ready, u - AHEAD)
                    sp.dma_start(x_in[s][:], x_units[u]).then_inc(x_loaded[s], 16)
                    wait_unit(sp, gated_ready, u - AHEAD)
                    sp.dma_start(og[s][:], out_gate[u]).then_inc(og_loaded[s], 16)

                each_unit(sp, UNITS, AHEAD, step)

            @block.tensor
            def _(pe):
                pe.wait_ge(ident_ready, 2)
                pe.wait_ge(weights_in, loads)

                def to_tokens(u, s):
                    wait_dma(pe, tri_loaded, u, s % 2)
                    wait_unit(pe, centred_ready, u - 2)
                    for t in range(TILES):
                        last = nc.tensor.transpose(tokens[s % 2][:, t, :], tri_in[s % 2][:, t * P:(t + 1) * P], ident[:])
                    last.then_inc(tokens_ready, 1)

                def project(u, s):
                    wait_unit(pe, gated_ready, u)
                    wait_unit(pe, x3_ready, u - 1)
                    for t in range(TILES):
                        last = nc.tensor.matmul(product[:, t, :], gated[s % 2][:, t * P:(t + 1) * P], w[:], start=True, stop=True)
                    last.then_inc(product_ready, 1)

                to_tokens(0, 0)
                to_tokens(1, 1)

                def step(u, s):
                    wait_unit(pe, centred_ready, u)
                    wait_unit(pe, normed_ready, u - 1)
                    for t in range(TILES):
                        last = nc.tensor.transpose(turned[:, t * P:(t + 1) * P], centred[s % 2][:, t, :], ident[:])
                    last.then_inc(turned_ready, 1)
                    if exists(u + 2, UNITS):
                        to_tokens(u + 2, s)
                    if exists(u - 1, UNITS):
                        project(u - 1, s + 1)

                each_unit(pe, UNITS, AHEAD, step)
                project(UNITS - 1, UNITS - 1)

            @block.vector
            def _(dve):
                def stats(u, s):
                    wait_unit(dve, tokens_ready, u)
                    tile_stats(nc, norm.stats[s % 2], tokens[s % 2], stats_ready)

                def finish(u, s):
                    wait_unit(dve, product_ready, u)
                    wait_unit(dve, x_b_ready, u)
                    wait_dma(dve, stored, u - 2, s % 2)
                    nc.vector.tensor_tensor(x3_sb[s % 2][:].rearrange("p t c -> p (t c)"),
                                            product[:].rearrange("p t c -> p (t c)"),
                                            x_b[s % 2][:].rearrange("p t c -> p (t c)"), ALU.add).then_inc(x3_ready, 1)

                def gating(u, s):
                    wait_unit(dve, normed_ready, u)
                    wait_dma(dve, og_loaded, u, s % AHEAD, AHEAD)
                    wait_unit(dve, product_ready, u - 2)
                    nc.vector.tensor_tensor(gated[s % 2][:], normed[s % 2][:], og[s % AHEAD][:], ALU.mult).then_inc(gated_ready, 1)

                stats(0, 0)

                def step(u, s):
                    if exists(u - 1, UNITS):
                        gating(u - 1, s + 3)
                    if exists(u + 1, UNITS):
                        stats(u + 1, s + 1)
                    wait_unit(dve, rstd_ready, u)
                    wait_unit(dve, turned_ready, u - 2)
                    norm.apply(nc, s % 2, centred[s % 2], tokens[s % 2], centred_ready)
                    if exists(u - 1, UNITS):
                        finish(u - 1, s + 3)

                each_unit(dve, UNITS, AHEAD, step)
                gating(UNITS - 1, UNITS - 1)
                finish(UNITS - 1, UNITS - 1)

            @block.gpsimd
            def _(pool):
                make_identity(nc, ident, ident_ready)
                norm.prepare(nc)
                pool.wait_ge(weights_in, loads)

                def step(u, s):
                    wait_unit(pool, stats_ready, u)
                    wait_unit(pool, centred_ready, u - 2)
                    norm.rstd_of(nc, u, s % 2, rstd_ready)
                    wait_dma(pool, x_loaded, u, s, AHEAD)
                    wait_unit(pool, x3_ready, u - 2)
                    nc.gpsimd.tensor_tensor(x_b[s % 2][:], x_in[s][:], b_all[:].unsqueeze(1).to_broadcast([P, TILES, C]),
                                            ALU.add).then_inc(x_b_ready, 1)

                each_unit(pool, UNITS, AHEAD, step)

            @block.scalar
            def _(act):
                act.wait_ge(weights_in, loads)

                def store(u, s):
                    wait_unit(act, x3_ready, u)
                    act.dma_start(x3_units[u], x3_sb[s % 2][:]).then_inc(stored[s % 2], 16)

                def step(u, s):
                    wait_unit(act, turned_ready, u)
                    wait_unit(act, gated_ready, u - 2)
                    for half in range(2):
                        cols = slice(half * BANK, (half + 1) * BANK)
                        last = nc.scalar.activation(normed[s % 2][:, cols], turned[:, cols], ACT.Identity,
                                                    scale=g_col[:, 0:1], bias=b_col[:, 0:1])
                    last.then_inc(normed_ready, 1)
                    if exists(u - 2, UNITS):
                        store(u - 2, s)

                each_unit(act, UNITS, AHEAD, step)
                for u in (UNITS - 2, UNITS - 1):
                    store(u, u)
                for s in range(2):
                    wait_dma(act, stored, UNITS - 2 + s, s)

        mem.clear()


def experts(nc, x3, router_w, router_b, expert_w, expert_b, x4):
    E, HALF_E = EXPERTS, EXPERTS // 2
    with ExitStack() as stack:
        mem = Memory(nc, stack, "moe")
        norm = RowNorm(mem, 1.0, EPS_T)
        x_in = [mem.sbuf(f"x{s}", [P, TILES, C]) for s in range(AHEAD)]
        centred = [mem.sbuf(f"centred{s}", [P, TILES, C]) for s in range(2)]
        xT = [mem.sbuf(f"xT{s}", [C, UNIT]) for s in range(2)]
        w_all = mem.sbuf("w_all", [C, E * C])
        w_router = mem.sbuf("w_router", [C, E])
        b_router = mem.sbuf("b_router", [P, E])
        b_blocks = mem.sbuf("b_blocks", [TILES * E, TILES, C])
        ident = mem.sbuf("ident", [P, P])
        logits = mem.sbuf("logits", [P, TILES, E])
        best = mem.sbuf("best", [P, TILES, 8])
        shifted, chosen, equal = (mem.sbuf(n, [P, TILES, E]) for n in ("shifted", "chosen", "equal"))
        rank = [mem.sbuf(f"rank{n}", [P, TILES, E]) for n in range(3)]
        diff, share, unscaled = (mem.sbuf(n, [P, TILES, E]) for n in ("diff", "share", "unscaled"))
        wait_tick = mem.sbuf("wait_tick", [P, 2])
        places, apart = mem.sbuf("places", [P, TILES]), mem.sbuf("apart", [P, TILES])
        total, inv = mem.sbuf("total", [P, TILES]), mem.sbuf("inv", [P, TILES])
        weight = [mem.sbuf(f"weight{s}", [P, TILES, E]) for s in range(2)]
        weightT = mem.sbuf("weightT", [TILES * E, P])
        acc = [mem.sbuf(f"acc{s}", [P, TILES, C]) for s in range(2)]
        upper = [mem.sbuf(f"upper{n}", [P, HALF_E, C]) for n in range(2)]
        pairs = [mem.sbuf(f"pairs{n}", [P, 2, C]) for n in range(2)]
        upper_sum = [mem.sbuf(f"upper_sum{n}", [P, C]) for n in range(2)]
        out = [mem.sbuf(f"out{s}", [P, TILES, C]) for s in range(2)]
        turned = mem.psum("turned", [C, UNIT])
        small = mem.psum("small", [P, TILES * E])
        small_turned = mem.psum("small_turned", [TILES * E, P])
        low = [mem.psum(f"low{n}", [P, HALF_E * C]) for n in range(2)]
        high = [mem.psum(f"high{n}", [P, HALF_E * C]) for n in range(2)]

        weights_in, ident_ready, blocks_zero = mem.sem("weights_in"), mem.sem("ident"), mem.sem("blocks_zero")
        x_loaded, stored = mem.sems("x_loaded", AHEAD), mem.sems("stored")
        (stats_ready, rstd_ready, centred_ready, turned_ready, xT_ready, logits_product, logits_ready, best_ready,
         exp_ready, route_step, total_ready, inv_ready, weight_ready, weight_turned, weightT_ready, bias_product,
         acc_ready, low_product, high_product, low_ready, high_ready, upper_step, upper_summed, low_step, chosen_ready, unscaled_ready) = (
            mem.sem(n) for n in ("stats", "rstd", "centred_ready", "turned_ready", "xT_ready", "logits_product",
                                 "logits_ready", "best_ready", "exp_ready", "route_step", "total_ready", "inv_ready",
                                 "weight_ready", "weight_turned", "weightT_ready", "bias_product", "acc_ready",
                                 "low_product", "high_product", "low_ready", "high_ready", "upper_step",
                                 "upper_summed", "low_step", "chosen_ready", "unscaled_ready"))
        loads = 16 * (E + 2 + TILES)
        x_units = x3.rearrange("(u t p) c -> u p t c", t=TILES, p=P)
        x4_units = x4.rearrange("(u t p) c -> u p t c", t=TILES, p=P)

        with nc.Block() as block:
            @block.sync
            def _(sp):
                for e in range(E):
                    sp.dma_start(w_all[:, e * C:(e + 1) * C], expert_w[e]).then_inc(weights_in, 16)
                sp.dma_start(w_router[:], router_w).then_inc(weights_in, 16)
                sp.dma_start(b_router[:], row_to_all(router_b)).then_inc(weights_in, 16)
                sp.wait_ge(blocks_zero, 1)
                for t in range(TILES):
                    sp.dma_start(b_blocks[t * E:(t + 1) * E, t, :], expert_b).then_inc(weights_in, 16)

                def step(u, s):
                    wait_unit(sp, acc_ready, u - AHEAD)
                    sp.dma_start(x_in[s][:], x_units[u]).then_inc(x_loaded[s], 16)

                each_unit(sp, UNITS, AHEAD, step)

            @block.tensor
            def _(pe):
                pe.wait_ge(ident_ready, 2)
                pe.wait_ge(weights_in, loads)

                def front(u, s):
                    wait_unit(pe, centred_ready, u)
                    wait_unit(pe, acc_ready, u - 1)
                    for t in range(TILES):
                        last = nc.tensor.transpose(turned[:, t * P:(t + 1) * P], centred[s % 2][:, t, :], ident[:])
                    last.then_inc(turned_ready, 1)
                    wait_unit(pe, xT_ready, u)
                    wait_unit(pe, logits_ready, u - 1)
                    for t in range(TILES):
                        last = nc.tensor.matmul(small[:, t * E:(t + 1) * E], xT[s % 2][:, t * P:(t + 1) * P], w_router[:],
                                                start=True, stop=True)
                    last.then_inc(logits_product, 1)

                def biases(u, s):
                    wait_alone(pe, weight_ready, u + 1, weights_in, loads)
                    nc.tensor.transpose(small_turned[:], weight[s % 2][:].rearrange("p t e -> p (t e)"), ident[:]
                                        ).then_inc(weight_turned, 1)
                    wait_unit(pe, weightT_ready, u)
                    for half in range(2):
                        last = nc.tensor.matmul(turned[:, half * BANK:(half + 1) * BANK], weightT[:],
                                                b_blocks[:, half * 4:(half + 1) * 4, :].rearrange("r t c -> r (t c)"),
                                                start=True, stop=True)
                    last.then_inc(bias_product, 1)

                def multiply(u, s, tiles):
                    for t in tiles:
                        lhs = xT[s % 2][:, t * P:(t + 1) * P]
                        wait_count(pe, low_ready, u * TILES + (t - 1))
                        nc.tensor.matmul(low[t % 2][:], lhs, w_all[:, 0:BANK], start=True, stop=True).then_inc(low_product, 1)
                        wait_count(pe, high_ready, u * TILES + (t - 1))
                        nc.tensor.matmul(high[t % 2][:], lhs, w_all[:, BANK:2 * BANK], start=True, stop=True
                                         ).then_inc(high_product, 1)

                front(0, 0)
                biases(0, 0)

                def step(u, s):
                    multiply(u, s, range(0, 2))
                    if exists(u + 1, UNITS):
                        front(u + 1, s + 1)
                    multiply(u, s, range(2, 6))
                    if exists(u + 1, UNITS):
                        biases(u + 1, s + 1)
                    multiply(u, s, range(6, 8))

                each_unit(pe, UNITS, AHEAD, step)

            @block.vector
            def _(dve):
                def stats(u, s):
                    wait_dma(dve, x_loaded, u, s % AHEAD, AHEAD)
                    tile_stats(nc, norm.stats[s % 2], x_in[s % AHEAD], stats_ready)

                def centre(u, s):
                    wait_unit(dve, rstd_ready, u)
                    wait_unit(dve, turned_ready, u - 2)
                    norm.apply(nc, s % 2, centred[s % 2], x_in[s % AHEAD], centred_ready)

                def route(u, s):
                    wait_unit(dve, logits_product, u)
                    wait_unit(dve, weight_ready, u - 1)
                    nc.vector.tensor_tensor(logits[:], small[:].rearrange("p (t e) -> p t e", e=E),
                                            b_router[:].unsqueeze(1).to_broadcast([P, TILES, E]), ALU.add
                                            ).then_inc(logits_ready, 1)
                    wait_alone(dve, logits_ready, u + 1, weights_in, loads)
                    for t in range(TILES):
                        last = nc.vector.max(out=best[:, t, :], in_=logits[:, t, :])
                    last.then_inc(best_ready, 1)

                def finish_weights(u, s):
                    wait_unit(dve, unscaled_ready, u)
                    nc.vector.tensor_reduce(out=total[:], in_=unscaled[:], axis=AX.X, op=ALU.add).then_inc(total_ready, 1)
                    wait_unit(dve, total_ready, u)
                    nc.vector.reciprocal(inv[:], total[:]).then_inc(inv_ready, 1)
                    wait_unit(dve, weight_turned, u)
                    wait_unit(dve, bias_product, u - 1)
                    nc.vector.tensor_copy(weightT[:], small_turned[:]).then_inc(weightT_ready, 1)

                def start_sum(u, s):
                    wait_unit(dve, bias_product, u)
                    wait_unit(dve, upper_summed, u - 2, per=TILES)
                    nc.vector.tensor_tensor(acc[s % 2][:].rearrange("p t c -> p (t c)"), turned[:],
                                            x_in[s % AHEAD][:].rearrange("p t c -> p (t c)"), ALU.add).then_inc(acc_ready, 1)

                def add_experts(u, s, tiles):
                    for t in tiles:
                        wait_count(dve, low_product, u * TILES + (t + 1))
                        if t == 0:
                            wait_unit(dve, acc_ready, u)
                            wait_unit(dve, weight_ready, u)
                        for e in range(HALF_E):
                            ins = nc.vector.scalar_tensor_tensor(
                                acc[s % 2][:, t, :], low[t % 2][:, e * C:(e + 1) * C], weight[s % 2][:, t, e:e + 1],
                                acc[s % 2][:, t, :], ALU.mult, ALU.add)
                            if e < HALF_E - 1:
                                ins.then_inc(low_step, 1)
                                wait_count(dve, low_step, u * (TILES * (HALF_E - 1)) + (t * (HALF_E - 1) + e + 1))
                            else:
                                ins.then_inc(low_ready, 1)

                dve.wait_ge(weights_in, loads)
                stats(0, 0)
                stats(1, 1)
                centre(0, 0)
                route(0, 0)
                finish_weights(0, 0)
                start_sum(0, 0)
                centre(1, 1)

                def step(u, s):
                    add_experts(u, s, range(0, 2))
                    if exists(u + 1, UNITS):
                        route(u + 1, s + 1)
                    if exists(u + 2, UNITS):
                        stats(u + 2, s + 2)
                    add_experts(u, s, range(2, 5))
                    if exists(u + 1, UNITS):
                        finish_weights(u + 1, s + 1)
                    add_experts(u, s, range(5, 6))
                    if exists(u + 2, UNITS):
                        centre(u + 2, s + 2)
                    if exists(u + 1, UNITS):
                        start_sum(u + 1, s + 1)
                    add_experts(u, s, range(6, 8))

                each_unit(dve, UNITS, AHEAD, step)

            @block.gpsimd
            def _(pool):
                nc.gpsimd.memset(b_blocks[:], 0.0).then_inc(blocks_zero, 1)
                make_identity(nc, ident, ident_ready)
                norm.prepare(nc)
                g = nc.gpsimd
                ROUTE = 8

                def norms(u, s):
                    wait_unit(pool, stats_ready, u)
                    wait_unit(pool, centred_ready, u - 2)
                    norm.rstd_of(nc, u, s % 2, rstd_ready)

                def choose(u, s):
                    done = [0]

                    def link(instruction, comparison=False):
                        instruction.then_inc(route_step, 1)
                        done[0] += 1
                        wait_count(pool, route_step, u * ROUTE + done[0])
                        if comparison:
                            g.tensor_tensor(wait_tick[:, done[0] % 2:done[0] % 2 + 1], norm.power[:, 0:1], norm.power[:, 0:1], ALU.add)

                    wait_unit(pool, best_ready, u)
                    g.tensor_tensor(apart[:], best[:, :, 0], best[:, :, 1], ALU.subtract)
                    g.tensor_tensor(diff[:], logits[:], best[:, :, 1:2].to_broadcast([P, TILES, E]), ALU.subtract)
                    link(g.tensor_tensor(shifted[:], logits[:], best[:, :, 0:1].to_broadcast([P, TILES, E]), ALU.subtract), True)
                    g.tensor_scalar(equal[:], diff[:], 0.0, 0.0, ALU.is_equal, ALU.add)
                    g.tensor_scalar(chosen[:], diff[:], 0.0, 0.0, ALU.is_gt, ALU.add)
                    link(g.tensor_scalar(places[:], apart[:], 0.0, 1.0, ALU.is_equal, ALU.add))
                    g.tensor_tensor(rank[0][:, :, 1:E], equal[:, :, 1:E], equal[:, :, 0:E - 1], ALU.add)
                    link(g.tensor_copy(rank[0][:, :, 0:1], equal[:, :, 0:1]))
                    g.tensor_tensor(rank[1][:, :, 2:E], rank[0][:, :, 2:E], rank[0][:, :, 0:E - 2], ALU.add)
                    link(g.tensor_copy(rank[1][:, :, 0:2], rank[0][:, :, 0:2]))
                    g.tensor_tensor(rank[2][:, :, 4:E], rank[1][:, :, 4:E], rank[1][:, :, 0:4], ALU.add)
                    link(g.tensor_copy(rank[2][:, :, 0:4], rank[1][:, :, 0:4]))
                    link(g.tensor_tensor(rank[0][:], rank[2][:], places[:].unsqueeze(2).to_broadcast([P, TILES, E]), ALU.subtract), True)
                    link(g.tensor_scalar(rank[1][:], rank[0][:], 0.0, 0.0, ALU.is_le, ALU.add))
                    link(g.tensor_tensor(rank[0][:], rank[1][:], equal[:], ALU.mult))
                    g.tensor_tensor(chosen[:], chosen[:], rank[0][:], ALU.add).then_inc(chosen_ready, 1)

                def weigh(u, s):
                    wait_unit(pool, exp_ready, u)
                    wait_unit(pool, chosen_ready, u)
                    g.tensor_tensor(unscaled[:], share[:], chosen[:], ALU.mult).then_inc(unscaled_ready, 1)
                    wait_unit(pool, inv_ready, u)
                    wait_unit(pool, unscaled_ready, u)
                    wait_unit(pool, low_ready, u - 2, per=TILES)
                    wait_unit(pool, high_ready, u - 2, per=TILES)
                    g.tensor_tensor(weight[s % 2][:], unscaled[:], inv[:].unsqueeze(2).to_broadcast([P, TILES, E]), ALU.mult
                                    ).then_inc(weight_ready, 1)

                def add_upper(u, s, tiles):
                    for t in tiles:
                        n = t % 2
                        wait_count(pool, high_ready, u * TILES + (t + 1))
                        g.tensor_tensor(pairs[n][:], upper[n][:, 0:2, :], upper[n][:, 2:4, :], ALU.add).then_inc(upper_step, 1)
                        wait_count(pool, upper_step, u * (2 * TILES) + (2 * t + 1))
                        g.tensor_tensor(upper_sum[n][:], pairs[n][:, 0, :], pairs[n][:, 1, :], ALU.add).then_inc(upper_step, 1)
                        wait_count(pool, upper_step, u * (2 * TILES) + (2 * t + 2))
                        wait_count(pool, low_ready, u * TILES + (t + 1))
                        if t == 0:
                            wait_dma(pool, stored, u - 2, s % 2)
                        g.tensor_tensor(out[s % 2][:, t, :], acc[s % 2][:, t, :], upper_sum[n][:], ALU.add
                                        ).then_inc(upper_summed, 1)

                norms(0, 0)
                norms(1, 1)
                choose(0, 0)
                weigh(0, 0)

                def step(u, s):
                    add_upper(u, s, range(0, 2))
                    if exists(u + 1, UNITS):
                        choose(u + 1, s + 1)
                        weigh(u + 1, s + 1)
                    add_upper(u, s, range(2, 5))
                    if exists(u + 2, UNITS):
                        norms(u + 2, s + 2)
                    add_upper(u, s, range(5, 8))

                each_unit(pool, UNITS, AHEAD, step)

            @block.scalar
            def _(act):
                act.wait_ge(weights_in, loads)

                def take_turned(u, s):
                    wait_unit(act, turned_ready, u)
                    wait_unit(act, high_product, u - 2, per=TILES)
                    for half in range(2):
                        cols = slice(half * BANK, (half + 1) * BANK)
                        last = nc.scalar.copy(xT[s % 2][:, cols], turned[:, cols])
                    last.then_inc(xT_ready, 1)

                def shares(u, s):
                    wait_unit(act, route_step, u, per=8, part=1)
                    wait_unit(act, unscaled_ready, u - 1)
                    nc.scalar.activation(share[:], shifted[:], ACT.Exp).then_inc(exp_ready, 1)

                def scale_upper(u, s, tiles):
                    for t in tiles:
                        n = t % 2
                        wait_count(act, high_product, u * TILES + (t + 1))
                        wait_count(act, upper_step, u * (2 * TILES) + (2 * t - 3))
                        if t == 0:
                            wait_unit(act, weight_ready, u)
                        for e in range(HALF_E):
                            last = nc.scalar.activation(upper[n][:, e, :], high[n][:, e * C:(e + 1) * C], ACT.Copy,
                                                        scale=weight[s % 2][:, t, HALF_E + e:HALF_E + e + 1])
                        last.then_inc(high_ready, 1)

                def store(u, s):
                    wait_unit(act, upper_summed, u, per=TILES)
                    act.dma_start(x4_units[u], out[s % 2][:]).then_inc(stored[s % 2], 16)

                take_turned(0, 0)
                shares(0, 0)

                def step(u, s):
                    scale_upper(u, s, range(0, 2))
                    if exists(u + 1, UNITS):
                        take_turned(u + 1, s + 1)
                    scale_upper(u, s, range(2, 3))
                    if exists(u - 1, UNITS):
                        store(u - 1, s + 1)
                    scale_upper(u, s, range(3, 4))
                    if exists(u + 1, UNITS):
                        shares(u + 1, s + 1)
                    scale_upper(u, s, range(4, 8))

                each_unit(act, UNITS, AHEAD, step)
                store(UNITS - 1, UNITS - 1)
                for s in range(2):
                    wait_dma(act, stored, UNITS - 2 + s, s)

        mem.clear()


def two_metaformer_layers(nc, a, out):
    def scratch(name, shape):
        return nc.dram_tensor(name, shape, F32, kind="Internal").ap()

    normed = scratch("normed", [ROWS, C, COLS])
    pair_bias = scratch("pair_bias", [HEADS, ROWS, COLS])
    x1, x2, x3 = (scratch(n, [TOKENS, C]) for n in ("x1", "x2", "x3"))
    wx, y, out_gate = (scratch(n, [UNITS, C, UNIT]) for n in ("wx", "y", "out_gate"))
    left, right, tri = (scratch(n, [C, PITCH]) for n in ("left", "right", "tri"))
    x = a["x"].rearrange("b i j c -> (b i j) c")
    x4 = out.rearrange("b i j c -> (b i j) c")
    bias_rows = pair_bias.rearrange("h j k -> h (j k)")
    l0, l1 = "L0_conv_", "L1_conv_"

    norm_project(nc, "norm", x, a[l0 + "Wb"], a[l0 + "ln_gamma"], a[l0 + "ln_beta"], normed,
                 lambda u: bias_rows[:, bass.ds(u * UNIT, UNIT)], HEADS, 1 + EPS_LN, EPS_C * EPS_LN)
    attention(nc, x, normed, pair_bias, *(a[l0 + n] for n in ("Wq", "Wk", "Wv", "Wg", "bg", "Wo", "bo")), x1)
    with nc.sbuf_tensor("wx_stats", [C, 2], F32) as wx_stats:
        norm_project(nc, "mix", x1, a["L0_ffn_W"], None, None, None, lambda u: wx[u], C, 1.0, EPS_T, wx_stats)
        recurrence(nc, wx, wx_stats, a["L0_ffn_V"], a["L0_ffn_gamma"], a["L0_ffn_beta"], y)
    names = ("lgate", "left", "rgate", "right", "ogate")
    gates(nc, x1, y, a[l1 + "norm_g"], a[l1 + "norm_b"], [a[l1 + n + "_w"] for n in names],
          [a[l1 + n + "_b"] for n in names], x2, left, right, out_gate)
    triangle(nc, left, right, tri)
    triangle_out(nc, tri, out_gate, x2, a[l1 + "onorm_g"], a[l1 + "onorm_b"], a[l1 + "to_out_w"], a[l1 + "to_out_b"], x3)
    experts(nc, x3, *(a["L1_ffn_" + n] for n in ("router_w", "router_b", "expert_w", "expert_b")), x4)


def kernel(**inputs):
    import concourse.bacc as bacc
    from concourse.bass_utils import run_bass_kernel_spmd

    nc = bacc.Bacc("TRN2", target_bir_lowering=False, num_devices=1)
    arrays, aps = {}, {}
    for name, value in inputs.items():
        value = np.ascontiguousarray(value)
        arrays[name] = value
        aps[name] = nc.dram_tensor(name, value.shape, mybir.dt.from_np(value.dtype), kind="ExternalInput").ap()
    out = nc.dram_tensor("x_out", inputs["x"].shape, F32, kind="ExternalOutput").ap()
    two_metaformer_layers(nc, aps, out)
    result = run_bass_kernel_spmd(nc, [arrays], core_ids=[0])
    return result.results[0]["x_out"]
```

```python
import numpy as np
import concourse.bass as bass
from concourse import mybir
from contextlib import ExitStack

F32 = mybir.dt.float32
F32R = mybir.dt.float32r
I32 = mybir.dt.int32
ALU = mybir.AluOpType
ACT = mybir.ActivationFunctionType
AX = mybir.AxisListType

P = 128
C = 128
ROWS = COLS = 256
TOKENS = ROWS * COLS
HEADS, HEAD_DIM = 4, 32
TILES = 8
UNIT = TILES * P
UNITS = TOKENS // UNIT
BANK = 512
PITCH = TOKENS + 1024
EPS_C, EPS_LN, EPS_T, EPS_BN = 1e-6, 1e-5, 1e-5, 1e-5
EXPERTS = 8
LOWEST = -3.0e38
AHEAD = 4


def each_unit(eng, units, slots, step):
    for s in range(slots):
        step(s, s)
    with eng.Fori(slots, units - slots, slots) as u:
        for s in range(slots):
            step(u + s if s else u, s)
    for s in range(slots):
        step(units - slots + s, s)


def exists(u, units):
    return not isinstance(u, int) or 0 <= u < units


def wait_count(eng, sem, n):
    if not isinstance(n, int) or n > 0:
        eng.wait_ge(sem, n)


def wait_alone(eng, sem, n, over, over_n):
    if isinstance(n, int):
        wait_count(eng, sem, n)
    else:
        value = eng.snap(n)
        eng.wait_ge(over, over_n)
        eng.wait_ge(sem, value)


def wait_unit(eng, sem, u, per=1, part=None):
    if not isinstance(u, int) or u >= 0:
        wait_count(eng, sem, u * per + (per if part is None else part))


def wait_dma(eng, sems, u, slot, slots=2):
    if not isinstance(u, int) or u >= 0:
        eng.wait_ge(sems[slot], (u - slot) * (16 // slots) + 16)


class Memory:

    def __init__(self, nc, stack, stage):
        self.nc, self.stack, self.stage, self.used = nc, stack, stage, []

    def sbuf(self, name, shape, dtype=F32):
        return self.stack.enter_context(self.nc.sbuf_tensor(f"{self.stage}_{name}", shape, dtype))

    def psum(self, name, shape):
        return self.stack.enter_context(self.nc.psum_tensor(f"{self.stage}_{name}", shape, F32))

    def sem(self, name):
        sem = self.stack.enter_context(self.nc.semaphore(f"{self.stage}_{name}"))
        self.used.append(sem)
        return sem

    def clear(self):
        with self.nc.Block() as block:
            @block.gpsimd
            def _(pool):
                for sem in self.used:
                    pool.sem_clear(sem)

    def sems(self, name, n=2):
        return [self.sem(f"{name}{i}") for i in range(n)]


def column(vector):
    return vector.rearrange("(c a) -> c a", a=1)


def row_to_all(vector, n=P):
    return vector.rearrange("(a c) -> a c", a=1).to_broadcast([n, vector.shape[0]])


def tile_stats(nc, stats, x, done):
    for t in range(TILES):
        last = nc.vector.bn_stats(stats[:, t, :], x[:, t, :])
    last.then_inc(done, 1)


class RowNorm:

    def __init__(self, mem, a, b, for_scalar=False):
        self.a, self.b = a, b
        self.steps = 5 if for_scalar else 4
        self.shift = [mem.sbuf(f"shift{s}", [P, TILES]) for s in range(2)] if for_scalar else None
        self.stats = [mem.sbuf(f"stats{s}", [P, TILES, 6]) for s in range(2)]
        self.mean = [mem.sbuf(f"mean{s}", [P, TILES]) for s in range(2)]
        self.rstd = [mem.sbuf(f"rstd{s}", [P, TILES]) for s in range(2)]
        self.tmp = [mem.sbuf(f"normtmp{i}", [P, TILES]) for i in range(6)]
        self.power = mem.sbuf("power", [P, TILES])
        self.quarter = mem.sbuf("quarter", [P, TILES])
        self.step_done = mem.sem("norm_step")

    def prepare(self, nc):
        nc.gpsimd.memset(self.quarter[:], self.a / 4)
        nc.gpsimd.memset(self.power[:], -0.5).then_inc(self.step_done, 1)
        nc.gpsimd.wait_ge(self.step_done, 1)

    def rstd_of(self, nc, u, s, ready):
        g, t = nc.gpsimd, self.tmp
        count_e = self.stats[s]
        mean_even, dev_even = count_e[:, :, 1], count_e[:, :, 2]
        mean_odd, dev_odd = count_e[:, :, 4], count_e[:, :, 5]
        base = u * self.steps + 1
        wait_unit(g, ready, u - 1)
        g.tensor_tensor(t[0][:], mean_even, mean_odd, ALU.add)
        g.tensor_tensor(t[1][:], mean_even, mean_odd, ALU.subtract)
        g.tensor_tensor(t[2][:], dev_even, dev_odd, ALU.add).then_inc(self.step_done, 1)
        g.wait_ge(self.step_done, base + 1)
        g.tensor_tensor(t[3][:], t[1][:], t[1][:], ALU.mult)
        g.tensor_scalar(self.mean[s][:], t[0][:], -0.5 if self.shift else 0.5, 0.0, ALU.mult, ALU.add)
        g.tensor_scalar(t[4][:], t[2][:], self.a / C, self.b, ALU.mult, ALU.add).then_inc(self.step_done, 1)
        g.wait_ge(self.step_done, base + 2)
        g.tensor_tensor(t[5][:], t[3][:], self.quarter[:], ALU.mult).then_inc(self.step_done, 1)
        g.wait_ge(self.step_done, base + 3)
        g.tensor_tensor(t[0][:], t[4][:], t[5][:], ALU.add).then_inc(self.step_done, 1)
        g.wait_ge(self.step_done, base + 4)
        rstd = g.tensor_tensor(self.rstd[s][:], t[0][:], self.power[:], ALU.pow)
        if self.shift is None:
            rstd.then_inc(ready, 1)
        else:
            rstd.then_inc(self.step_done, 1)
            g.wait_ge(self.step_done, base + 5)
            g.tensor_tensor(self.shift[s][:], self.mean[s][:], self.rstd[s][:], ALU.mult).then_inc(ready, 1)

    def apply(self, nc, s, out, x, done, tiles=range(TILES)):
        for t in tiles:
            last = nc.vector.tensor_scalar(out[:, t, :], x[:, t, :], self.mean[s][:, t:t + 1],
                                           self.rstd[s][:, t:t + 1], ALU.add if self.shift else ALU.subtract, ALU.mult)
        last.then_inc(done, 1)

    def apply_on_scalar(self, nc, s, out, x, done, tiles=range(TILES)):
        for t in tiles:
            last = nc.scalar.activation(out[:, t, :], x[:, t, :], ACT.Identity, scale=self.rstd[s][:, t:t + 1],
                                        bias=self.shift[s][:, t:t + 1])
        last.then_inc(done, 1)


def make_identity(nc, ident, sem, value=1.0):
    nc.gpsimd.memset(ident[:], 0.0).then_inc(sem, 1)
    nc.gpsimd.wait_ge(sem, 1)
    nc.gpsimd.affine_select(out=ident[:], in_=ident[:], compare_op=ALU.not_equal, fill=value, base=0,
                            pattern=[[-1, P]], channel_multiplier=1).then_inc(sem, 1)


def split_matmul(nc, out, lhsT, rhs):
    nc.tensor.matmul(out, lhsT[0], rhs[0], start=True, stop=False)
    nc.tensor.matmul(out, lhsT[0], rhs[1], start=False, stop=False)
    return nc.tensor.matmul(out, lhsT[1], rhs[0], start=False, stop=True)


def norm_project(nc, stage, x, weight, gamma, beta, normed, projected, out_rows, a, b, wx_stats=None):
    DEEP, LAG = 8, 6
    with ExitStack() as stack:
        mem = Memory(nc, stack, stage)
        norm = RowNorm(mem, a, b, for_scalar=True)
        x_in = [mem.sbuf(f"x{s}", [P, TILES, C]) for s in range(DEEP)]
        centred = [mem.sbuf(f"centred{s}", [P, TILES, C]) for s in range(2)]
        xT = [mem.sbuf(f"xT{s}", [C, UNIT]) for s in range(2)]
        result = [mem.sbuf(f"result{s}", [out_rows, UNIT]) for s in range(2)]
        w_raw = mem.sbuf("w_raw", [C, out_rows])
        w = mem.sbuf("w", [C, out_rows])
        ident = mem.sbuf("ident", [P, P])
        g_col, b_col = mem.sbuf("g_col", [C, 1]), mem.sbuf("b_col", [C, 1])
        turned = [mem.psum(f"turned{s}", [C, UNIT]) for s in range(2)]
        product = [mem.psum(f"product{s}", [out_rows, UNIT]) for s in range(2)]
        if wx_stats is not None:
            batch = mem.sbuf("batch", [out_rows, 2 * UNITS, 6])

        weights_in, ident_ready, w_ready, w_turned = (mem.sem(n) for n in ("weights_in", "ident", "w_ready", "w_turned"))
        x_loaded, normed_out, result_out = mem.sems("x_loaded", DEEP), mem.sems("normed_out"), mem.sems("result_out")
        stats_ready, rstd_ready, centred_low, centred_high = (
            mem.sem(n) for n in ("stats", "rstd", "centred_low", "centred_high"))
        cut = TILES // 2 if wx_stats is not None else TILES - 2
        LOW_TILES, HIGH_TILES = range(cut), range(cut, TILES)
        turned_ready, xT_ready, product_ready, result_ready, batch_ready = (
            mem.sem(n) for n in ("turned_ready", "xT_ready", "product_ready", "result_ready", "batch_ready"))
        loads = 16 * (1 + 2 * (gamma is not None))
        x_units = x.rearrange("(u t p) c -> u p t c", t=TILES, p=P)

        with nc.Block() as block:
            @block.sync
            def _(sp):
                sp.dma_start(w_raw[:], weight).then_inc(weights_in, 16)
                if gamma is not None:
                    sp.dma_start(g_col[:], column(gamma)).then_inc(weights_in, 16)
                    sp.dma_start(b_col[:], column(beta)).then_inc(weights_in, 16)

                def step(u, s):
                    wait_unit(sp, centred_low, u - DEEP)
                    wait_unit(sp, centred_high, u - DEEP)
                    sp.dma_start(x_in[s][:], x_units[u]).then_inc(x_loaded[s], 16)
                    if exists(u - LAG, UNITS):
                        store(u - LAG, s % 2)

                def store(u, s):
                    wait_unit(sp, result_ready, u)
                    sp.dma_start(projected(u), result[s][:]).then_inc(result_out[s], 16)

                each_unit(sp, UNITS, DEEP, step)
                for u in range(UNITS - LAG, UNITS):
                    store(u, u % 2)
                for s in range(2):
                    wait_dma(sp, result_out, UNITS - 2 + s, s)

            @block.vector
            def _(dve):
                def stats(u, s):
                    wait_dma(dve, x_loaded, u, s, DEEP)
                    wait_unit(dve, rstd_ready, u - 2)
                    tile_stats(nc, norm.stats[s % 2], x_in[s], stats_ready)

                if wx_stats is not None:
                    dve.wait_ge(w_turned, 1)
                    nc.vector.tensor_copy(w[:], turned[0][:, 0:out_rows]).then_inc(w_ready, 1)
                else:
                    dve.wait_ge(weights_in, loads)
                    nc.vector.tensor_copy(w[:], w_raw[:]).then_inc(w_ready, 1)

                def centre(u, s):
                    wait_unit(dve, rstd_ready, u)
                    wait_unit(dve, turned_ready, u - 2)
                    norm.apply(nc, s % 2, centred[s % 2], x_in[s], centred_low, LOW_TILES)

                stats(0, 0)
                stats(1, 1)
                centre(0, 0)

                def batch_stats(u, s):
                    wait_unit(dve, result_ready, u)
                    for half in range(2):
                        last = nc.vector.bn_stats(batch[:, bass.ds(u * 2 + half, 1), :],
                                                  result[s][:, half * BANK:(half + 1) * BANK])
                    last.then_inc(batch_ready, 1)

                def step(u, s):
                    if exists(u + 2, UNITS):
                        stats(u + 2, (s + 2) % DEEP)
                    if exists(u + 1, UNITS):
                        centre(u + 1, (s + 1) % DEEP)
                    if wx_stats is not None and exists(u - 2, UNITS):
                        batch_stats(u - 2, s % 2)

                each_unit(dve, UNITS, DEEP, step)
                if wx_stats is not None:
                    for u in (UNITS - 2, UNITS - 1):
                        batch_stats(u, u % 2)
                    dve.wait_ge(batch_ready, UNITS)
                    nc.vector.bn_aggr(wx_stats[:], batch[:].rearrange("p n k -> p (n k)"))

            @block.gpsimd
            def _(pool):
                make_identity(nc, ident, ident_ready)
                norm.prepare(nc)

                def step(u, s):
                    wait_unit(pool, stats_ready, u)
                    wait_unit(pool, centred_low, u - 2)
                    wait_unit(pool, centred_high, u - 2)
                    norm.rstd_of(nc, u, s, rstd_ready)

                each_unit(pool, UNITS, 2, step)

            @block.tensor
            def _(pe):
                pe.wait_ge(ident_ready, 2)
                pe.wait_ge(weights_in, loads)
                if wx_stats is not None:
                    nc.tensor.transpose(turned[0][:, 0:out_rows], w_raw[:], ident[:]).then_inc(w_turned, 1)
                pe.wait_ge(w_ready, 1)

                def multiply(u, s):
                    wait_unit(pe, xT_ready, u)
                    wait_unit(pe, result_ready, u - 2)
                    for half in range(2):
                        cols = slice(half * BANK, (half + 1) * BANK)
                        last = nc.tensor.matmul(product[s][:, cols], w[:], xT[s][:, cols], start=True, stop=True)
                    last.then_inc(product_ready, 1)

                def step(u, s):
                    wait_unit(pe, centred_low, u)
                    wait_unit(pe, centred_high, u)
                    wait_unit(pe, xT_ready, u - 2)
                    for t in range(TILES):
                        last = nc.tensor.transpose(turned[s][:, t * P:(t + 1) * P], centred[s][:, t, :], ident[:])
                    last.then_inc(turned_ready, 1)
                    if exists(u - 1, UNITS):
                        multiply(u - 1, 1 - s)

                each_unit(pe, UNITS, 2, step)
                multiply(UNITS - 1, (UNITS - 1) % 2)

            @block.scalar
            def _(act):
                act.wait_ge(weights_in, loads)
                if wx_stats is not None:
                    act.wait_ge(w_ready, 1)

                def store_result(u, s):
                    wait_unit(act, product_ready, u)
                    wait_dma(act, result_out, u - 2, s)
                    if wx_stats is not None:
                        wait_unit(act, batch_ready, u - 2)
                    for half in range(2):
                        cols = slice(half * BANK, (half + 1) * BANK)
                        last = nc.scalar.copy(result[s][:, cols], product[s][:, cols])
                    last.then_inc(result_ready, 1)


                def centre(u, s):
                    wait_dma(act, x_loaded, u, s, DEEP)
                    wait_unit(act, rstd_ready, u)
                    wait_unit(act, turned_ready, u - 2)
                    norm.apply_on_scalar(nc, s % 2, centred[s % 2], x_in[s], centred_high, HIGH_TILES)

                def take_turned(u, s):
                    wait_unit(act, turned_ready, u)
                    wait_unit(act, product_ready, u - 2)
                    if normed is not None:
                        wait_dma(act, normed_out, u - 2, s)
                    for half in range(2):
                        cols = slice(half * BANK, (half + 1) * BANK)
                        if gamma is not None:
                            last = nc.scalar.activation(xT[s][:, cols], turned[s][:, cols], ACT.Identity,
                                                        scale=g_col[:, 0:1], bias=b_col[:, 0:1])
                        else:
                            last = nc.scalar.copy(xT[s][:, cols], turned[s][:, cols])
                    last.then_inc(xT_ready, 1)

                centre(0, 0)

                def step(u, s):
                    if exists(u + 1, UNITS):
                        centre(u + 1, (s + 1) % DEEP)
                    take_turned(u, s % 2)
                    if exists(u - 1, UNITS):
                        store_result(u - 1, (s + 1) % 2)
                    if normed is not None:
                        wait_unit(act, xT_ready, u)
                        act.dma_start(normed[bass.ds(u * (UNIT // COLS), UNIT // COLS)].rearrange("r c t -> c r t"),
                                      xT[s % 2][:].rearrange("c (r t) -> c r t", t=COLS)).then_inc(normed_out[s % 2], 16)

                each_unit(act, UNITS, DEEP, step)
                if normed is not None:
                    for s in range(2):
                        wait_dma(act, normed_out, UNITS - 2 + s, s)
                store_result(UNITS - 1, (UNITS - 1) % 2)

        mem.clear()


def attention(nc, x, normed, pair_bias, Wq, Wk, Wv, Wg, bg, Wo, bo, x1):
    scale = 1.0 / float(np.sqrt(HEAD_DIM))
    with ExitStack() as stack:
        mem = Memory(nc, stack, "att")
        xT = [mem.sbuf(f"xT{s}", [C, COLS]) for s in range(AHEAD)]
        x_res = [mem.sbuf(f"x_res{s}", [P, 2, C]) for s in range(AHEAD)]
        qk = [[mem.sbuf(f"qk_{part}{s}", [C, 2, COLS], F32R) for part in ("high", "low")] for s in range(2)]
        xT_parts = [[mem.sbuf(f"xT_{part}{s}", [C, COLS], F32R) for part in ("high", "low")] for s in range(2)]
        w_parts = {n: [mem.sbuf(f"w_{n}_{part}", [C, C], F32R) for part in ("high", "low")] for n in "qkvg"}
        v = [mem.sbuf(f"v{s}", [P, 2, C]) for s in range(AHEAD)]
        gate = [mem.sbuf(f"gate{s}", [C, COLS]) for s in range(AHEAD)]
        probs = [mem.sbuf(f"probs{s}", [P, HEADS, 2, COLS]) for s in range(2)]
        top = [mem.sbuf(f"top{s}", [P, HEADS * 2]) for s in range(2)]
        neg_top = [mem.sbuf(f"neg_top{s}", [P, HEADS * 2]) for s in range(2)]
        total = [mem.sbuf(f"total{s}", [P, HEADS * 2]) for s in range(2)]
        inv = [mem.sbuf(f"inv{s}", [P, HEADS * 2]) for s in range(2)]
        probsT = mem.sbuf("probsT", [P, HEADS, 2, COLS])
        gate_inv = mem.sbuf("gate_inv", [C, COLS])
        valuesT = [mem.sbuf(f"valuesT{s}", [C, COLS]) for s in range(2)]
        x_bo = [mem.sbuf(f"x_bo{s}", [P, 2, C]) for s in range(2)]
        x1_out = [mem.sbuf(f"x1_out{s}", [P, 2, C]) for s in range(2)]
        bias = mem.sbuf("bias", [P, HEADS, 2, COLS])
        w = {n: mem.sbuf(f"w_{n}", [C, C]) for n in ("q", "k", "v", "g", "o", "q_raw")}
        bg_col, half_bg, bo_all = mem.sbuf("bg_col", [C, 1]), mem.sbuf("half_bg", [C, 1]), mem.sbuf("bo_all", [P, C])
        zeros = mem.sbuf("zeros", [C, COLS])
        wait_tick = mem.sbuf("wait_tick", [P, HEADS])
        ident, half_ident = mem.sbuf("ident", [P, P]), mem.sbuf("half_ident", [P, P])

        scores = [mem.psum(f"scores{h}", [P, 2, COLS]) for h in range(HEADS)]
        bank_a, bank_b, bank_c, bank_d = (mem.psum(f"bank_{n}", [P, 2, COLS]) for n in "abcd")

        weights_in, ident_ready, w_ready = mem.sem("weights_in"), mem.sem("ident"), mem.sem("w_ready")
        xT_loaded, res_loaded, x1_stored = mem.sems("xT_loaded", AHEAD), mem.sems("res_loaded", AHEAD), mem.sems("x1_stored")
        (xT_high, xT_split, projected, gv_projected, qk_high, qk_ready, gv_ready, scored, biased, neg_ready, exp_ready, inv_ready, turned, even_ready,
         odd_ready, inv_turned, gate_inv_ready, valued, valuesT_ready, out_ready, x_bo_ready, x1_ready) = (
            mem.sem(n) for n in ("xT_high", "xT_split", "projected", "gv_projected", "qk_high", "qk_ready", "gv_ready", "scored", "biased", "neg_ready", "exp_ready",
                                 "inv_ready", "turned", "even_ready", "odd_ready", "inv_turned", "gate_inv_ready",
                                 "valued", "valuesT_ready", "out_ready", "x_bo_ready", "x1_ready"))
        x_rows = x.rearrange("(i t p) c -> i p t c", t=2, p=P)
        x1_rows = x1.rearrange("(i t p) c -> i p t c", t=2, p=P)
        loads = 16 * 9

        with nc.Block() as block:
            @block.sync
            def _(sp):
                for name, src in (("q_raw", Wq), ("k", Wk), ("v", Wv), ("g", Wg), ("o", Wo)):
                    sp.dma_start(w[name][:], src).then_inc(weights_in, 16)
                sp.dma_start(bg_col[:], column(bg)).then_inc(weights_in, 16)
                sp.dma_start(bo_all[:], row_to_all(bo)).then_inc(weights_in, 16)
                for t in range(2):
                    sp.dma_start(bias[:, :, t, :], pair_bias[:, t * P:(t + 1) * P, :].rearrange("h p k -> p h k")
                                 ).then_inc(weights_in, 16)

                def step(i, s):
                    wait_unit(sp, xT_split, i - AHEAD)
                    sp.dma_start(xT[s][:], normed[i]).then_inc(xT_loaded[s], 16)
                    wait_unit(sp, x_bo_ready, i - AHEAD)
                    sp.dma_start(x_res[s][:], x_rows[i]).then_inc(res_loaded[s], 16)

                each_unit(sp, ROWS, AHEAD, step)

            @block.tensor
            def _(pe):
                pe.wait_ge(w_ready, 4)
                pe.wait_ge(ident_ready, 4)

                def project_gv(i, s):
                    wait_unit(pe, gv_ready, i - 1)
                    wait_unit(pe, gate_inv_ready, i - 3)
                    x_cols = [part[:] for part in xT_parts[s % 2]]
                    split_matmul(nc, bank_b[:, 0, :], [part[:] for part in w_parts["g"]], x_cols)
                    for t in range(2):
                        last = split_matmul(nc, bank_b[:, 1, t * P:(t + 1) * P], [x[:, t * P:(t + 1) * P] for x in x_cols],
                                            [part[:] for part in w_parts["v"]])
                    last.then_inc(gv_projected, 1)

                def project_qk(i, s):
                    wait_unit(pe, xT_split, i)
                    wait_unit(pe, even_ready, i - 3, per=2)
                    wait_unit(pe, qk_ready, i - 1)
                    for n, name in enumerate("qk"):
                        last = split_matmul(nc, bank_a[:, n, :], [part[:] for part in w_parts[name]],
                                            [part[:] for part in xT_parts[s % 2]])
                    last.then_inc(projected, 1)

                def score(i, s, heads):
                    wait_unit(pe, qk_ready, i)
                    for h in heads:
                        rows = slice(h * HEAD_DIM, (h + 1) * HEAD_DIM)
                        wait_unit(pe, biased, i - 1, per=HEADS, part=h + 1)
                        for t in range(2):
                            last = split_matmul(nc, scores[h][:, t, :], [part[rows, 0, t * P:(t + 1) * P] for part in qk[s % 2]],
                                                [part[rows, 1, :] for part in qk[s % 2]])
                        last.then_inc(scored, 1)

                def turn(i, s, heads):
                    for h in heads:
                        wait_unit(pe, exp_ready, i, per=HEADS, part=h + 1)
                        if h == 0:
                            newest = max((n for n in range(3) if exists(i + n, ROWS)))
                            wait_unit(pe, qk_ready, i + newest)
                        elif h == 2:
                            wait_unit(pe, even_ready, i, per=2, part=1)
                        elif h == 1:
                            wait_unit(pe, odd_ready, i - 1, per=2)
                        else:
                            wait_unit(pe, odd_ready, i, per=2, part=1)
                        bank = bank_c if h % 2 else bank_a
                        for k in range(2):
                            for t in range(2):
                                last = nc.tensor.transpose(bank[:, k, t * P:(t + 1) * P],
                                                           probs[s % 2][:, h, t, k * P:(k + 1) * P], ident[:])
                        last.then_inc(turned, 1)

                def turn_inv(i, s):
                    wait_unit(pe, inv_ready, i)
                    newest = max((n for n in range(3) if exists(i + n, ROWS)))
                    wait_unit(pe, gv_ready, i + newest)
                    for t in range(2):
                        for h in range(HEADS):
                            n = h * 2 + t
                            last = nc.tensor.matmul(bank_b[h * HEAD_DIM:(h + 1) * HEAD_DIM, 0, t * P:(t + 1) * P],
                                                    inv[s % 2][:, n:n + 1].to_broadcast([P, HEAD_DIM]), half_ident[:],
                                                    start=True, stop=True)
                    last.then_inc(inv_turned, 1)

                def values(i, s):
                    wait_unit(pe, odd_ready, i, per=2)
                    wait_unit(pe, even_ready, i, per=2)
                    wait_unit(pe, x1_ready, i - 1)
                    for k in range(2):
                        for h in range(HEADS):
                            rows = slice(h * HEAD_DIM, (h + 1) * HEAD_DIM)
                            last = nc.tensor.matmul(bank_d[rows, 0, :], v[s][:, k, rows], probsT[:, h, k, :],
                                                    start=(k == 0), stop=(k == 1))
                    last.then_inc(valued, 1)

                def project_out(i, s):
                    wait_unit(pe, valuesT_ready, i)
                    for t in range(2):
                        last = nc.tensor.matmul(bank_d[:, 1, t * P:(t + 1) * P], valuesT[s % 2][:, t * P:(t + 1) * P],
                                                w["o"][:], start=True, stop=True)
                    last.then_inc(out_ready, 1)

                project_qk(0, 0)
                project_gv(0, 0)
                score(0, 0, range(HEADS))
                for i in (1, 2):
                    project_qk(i, i)
                    project_gv(i, i)

                def step(i, s):
                    if exists(i + 1, ROWS):
                        score(i + 1, (s + 1) % AHEAD, (0,))
                    if exists(i - 1, ROWS):
                        project_out(i - 1, (s - 1) % AHEAD)
                    if exists(i + 1, ROWS):
                        score(i + 1, (s + 1) % AHEAD, (1,))
                    turn(i, s, (0, 1))
                    if exists(i + 1, ROWS):
                        score(i + 1, (s + 1) % AHEAD, (2, 3))
                    turn(i, s, (2, 3))
                    turn_inv(i, s)
                    if exists(i + 3, ROWS):
                        project_qk(i + 3, (s + 3) % AHEAD)
                    values(i, s)
                    if exists(i + 3, ROWS):
                        project_gv(i + 3, (s + 3) % AHEAD)

                each_unit(pe, ROWS, AHEAD, step)
                project_out(ROWS - 1, AHEAD - 1)

            @block.vector
            def _(dve):
                dve.wait_ge(weights_in, loads)
                nc.vector.tensor_scalar(half_bg[:], bg_col[:], 0.5, None, ALU.mult).then_inc(w_ready, 1)
                nc.vector.tensor_scalar(w["q"][:], w["q_raw"][:], scale, None, ALU.mult).then_inc(w_ready, 1)
                dve.wait_ge(w_ready, 2)
                for name, parts in w_parts.items():
                    last = nc.vector.tensor_copy(parts[0][:], w[name][:])
                last.then_inc(w_ready, 1)
                dve.wait_ge(w_ready, 3)
                for name, parts in w_parts.items():
                    last = nc.vector.tensor_tensor(parts[1][:], w[name][:], parts[0][:], ALU.subtract)
                last.then_inc(w_ready, 1)
                dve.wait_ge(ident_ready, 4)

                def take_low(i, s):
                    wait_unit(dve, qk_high, i)
                    nc.vector.tensor_tensor(qk[s % 2][1][:], bank_a[:], qk[s % 2][0][:], ALU.subtract).then_inc(qk_ready, 1)

                def add_bias(i, s, heads):
                    for h in heads:
                        if h == 0:
                            wait_unit(dve, turned, i - 2, per=HEADS)
                        wait_unit(dve, scored, i, per=HEADS, part=h + 1)
                        nc.vector.tensor_copy(wait_tick[:, h:h + 1], bg_col[:])
                        for t in range(2):
                            n = h * 2 + t
                            last = nc.vector.tensor_tensor_reduce(
                                out=probs[s % 2][:, h, t, :], in0=scores[h][:, t, :], in1=bias[:, h, t, :], scale=1.0,
                                scalar=LOWEST, op0=ALU.add, op1=ALU.max, accum_out=top[s % 2][:, n:n + 1])
                        last.then_inc(biased, 1)
                        if h % 2:
                            n = slice(h * 2 - 2, h * 2 + 2)
                            wait_unit(dve, biased, i, per=HEADS, part=h + 1)
                            nc.vector.tensor_scalar(neg_top[s % 2][:, n], top[s % 2][:, n], -1.0, None, ALU.mult
                                                    ).then_inc(neg_ready, 1)

                def take_even(i, part):
                    wait_unit(dve, turned, i, per=HEADS, part=2 * part + 1)
                    if part == 0:
                        wait_unit(dve, valued, i - 1)
                    nc.vector.tensor_copy(probsT[:, 2 * part], bank_a[:]).then_inc(even_ready, 1)

                def finish_row(i, s):
                    wait_unit(dve, out_ready, i)
                    wait_unit(dve, x_bo_ready, i)
                    wait_dma(dve, x1_stored, i - 2, s % 2)
                    nc.vector.tensor_tensor(x1_out[s % 2][:].rearrange("p t c -> p (t c)"), bank_d[:, 1, :],
                                            x_bo[s % 2][:].rearrange("p t c -> p (t c)"), ALU.add).then_inc(x1_ready, 1)

                take_low(0, 0)
                add_bias(0, 0, range(HEADS))
                take_low(1, 1)
                take_low(2, 2)

                def step(i, s):
                    more = exists(i + 1, ROWS)
                    if more:
                        add_bias(i + 1, (s + 1) % AHEAD, (0,))
                    take_even(i, 0)
                    if more:
                        add_bias(i + 1, (s + 1) % AHEAD, (1, 2))
                    wait_unit(dve, exp_ready, i, per=HEADS)
                    nc.vector.reciprocal(inv[s % 2][:], total[s % 2][:]).then_inc(inv_ready, 1)
                    take_even(i, 1)
                    if exists(i - 1, ROWS):
                        finish_row(i - 1, (s - 1) % AHEAD)
                    wait_unit(dve, inv_turned, i)
                    wait_unit(dve, gv_ready, i)
                    nc.vector.scalar_tensor_tensor(gate_inv[:], gate[s][:], 1.0, bank_b[:, 0, :], ALU.add, ALU.mult
                                                   ).then_inc(gate_inv_ready, 1)
                    if more:
                        add_bias(i + 1, (s + 1) % AHEAD, (3,))
                    wait_unit(dve, valued, i)
                    wait_unit(dve, gate_inv_ready, i)
                    nc.vector.tensor_tensor(valuesT[s % 2][:], bank_d[:, 0, :], gate_inv[:], ALU.mult
                                            ).then_inc(valuesT_ready, 1)
                    if exists(i + 3, ROWS):
                        take_low(i + 3, (s + 3) % AHEAD)

                each_unit(dve, ROWS, AHEAD, step)
                finish_row(ROWS - 1, AHEAD - 1)

            @block.gpsimd
            def _(pool):
                make_identity(nc, ident, ident_ready)
                pool.wait_ge(ident_ready, 2)
                nc.gpsimd.memset(half_ident[:], 0.0).then_inc(ident_ready, 1)
                pool.wait_ge(ident_ready, 3)
                nc.gpsimd.affine_select(out=half_ident[:], in_=half_ident[:], compare_op=ALU.not_equal, fill=0.5, base=0,
                                        pattern=[[-1, P]], channel_multiplier=1).then_inc(ident_ready, 1)
                nc.gpsimd.memset(zeros[:], 0.0).then_inc(ident_ready, 1)
                pool.wait_ge(ident_ready, 5)
                pool.wait_ge(weights_in, loads)

                def split(i, s):
                    wait_dma(pool, xT_loaded, i, s, AHEAD)
                    wait_unit(pool, gv_projected, i - 2)
                    nc.gpsimd.tensor_tensor(xT_parts[s % 2][0][:], xT[s][:], zeros[:], ALU.add).then_inc(xT_high, 1)
                    wait_unit(pool, xT_high, i)
                    nc.gpsimd.tensor_tensor(xT_parts[s % 2][1][:], xT[s][:], xT_parts[s % 2][0][:], ALU.subtract
                                            ).then_inc(xT_split, 1)

                for i in range(3):
                    split(i, i)

                def step(i, s):
                    if exists(i + 3, ROWS):
                        split(i + 3, (s + 3) % AHEAD)
                    wait_dma(pool, res_loaded, i, s, AHEAD)
                    wait_unit(pool, x1_ready, i - 2)
                    nc.gpsimd.tensor_tensor(x_bo[s % 2][:], x_res[s][:], bo_all[:].unsqueeze(1).to_broadcast([P, 2, C]),
                                            ALU.add).then_inc(x_bo_ready, 1)

                each_unit(pool, ROWS, AHEAD, step)

            @block.scalar
            def _(act):
                act.wait_ge(w_ready, 2)
                act.wait_ge(ident_ready, 4)

                def take_qk(i, s):
                    wait_unit(act, projected, i)
                    wait_unit(act, scored, i - 2, per=HEADS)
                    nc.scalar.copy(qk[s % 2][0][:], bank_a[:]).then_inc(qk_high, 1)

                def take_gv(i, s):
                    wait_unit(act, gv_projected, i)
                    nc.scalar.activation(gate[s][:], bank_b[:, 0, :], ACT.Tanh, scale=0.5, bias=half_bg[:, 0:1])
                    nc.scalar.copy(v[s][:].rearrange("p t c -> p (t c)"), bank_b[:, 1, :]).then_inc(gv_ready, 1)

                def exponentials(i, s, heads):
                    for h in heads:
                        wait_unit(act, neg_ready, i, per=2, part=h // 2 + 1)
                        if h == 0:
                            wait_unit(act, inv_ready, i - 2)
                        for t in range(2):
                            n = h * 2 + t
                            last = nc.scalar.activation(probs[s % 2][:, h, t, :], probs[s % 2][:, h, t, :], ACT.Exp,
                                                        bias=neg_top[s % 2][:, n:n + 1],
                                                        accum_out=total[s % 2][:, n:n + 1])
                        last.then_inc(exp_ready, 1)

                def take_odd(i, part):
                    wait_unit(act, turned, i, per=HEADS, part=2 * part + 2)
                    if part == 0:
                        wait_unit(act, valued, i - 1)
                    nc.scalar.copy(probsT[:, 2 * part + 1], bank_c[:]).then_inc(odd_ready, 1)

                for i in range(3):
                    take_qk(i, i)
                    take_gv(i, i)
                exponentials(0, 0, (0, 1))

                def step(i, s):
                    exponentials(i, s, (2, 3))
                    for part in range(2):
                        take_odd(i, part)
                    if exists(i + 1, ROWS):
                        exponentials(i + 1, (s + 1) % AHEAD, (0,))
                    if exists(i + 3, ROWS):
                        take_qk(i + 3, (s + 3) % AHEAD)
                    if exists(i + 1, ROWS):
                        exponentials(i + 1, (s + 1) % AHEAD, (1,))
                    if exists(i + 3, ROWS):
                        take_gv(i + 3, (s + 3) % AHEAD)
                    if exists(i - 1, ROWS):
                        store(i - 1, (s - 1) % AHEAD)

                def store(i, s):
                    wait_unit(act, x1_ready, i)
                    act.dma_start(x1_rows[i], x1_out[s % 2][:]).then_inc(x1_stored[s % 2], 16)

                each_unit(act, ROWS, AHEAD, step)
                store(ROWS - 1, AHEAD - 1)
                for s in range(2):
                    wait_dma(act, x1_stored, ROWS - 2 + s, s)

        mem.clear()



CHUNK = 64
HALVES = 2
HALF = TOKENS // HALVES
CHUNKS = HALF // CHUNK
GROUPS = 4
LANES = CHUNKS // GROUPS
WARM = 16
TOLERANCE = 2.0 ** -21


def recurrence(nc, wx, wx_stats, V, gamma, beta, y_out):
    with ExitStack() as stack:
        mem = Memory(nc, stack, "rec")
        steps = mem.sbuf("steps", [C, HALF])
        lanes = steps[:].rearrange("c (g n k) -> c g n k", g=GROUPS, k=CHUNK)
        first = mem.sbuf("first", [C, CHUNKS + 1])
        warm = [[mem.sbuf(f"warm{g}{p}", [C, LANES]) for p in range(2)] for g in range(GROUPS)]
        z = [mem.sbuf(f"z{g}", [C, LANES]) for g in range(GROUPS)]
        vT, v_raw, ident = mem.sbuf("vT", [C, C]), mem.sbuf("v_raw", [C, C]), mem.sbuf("ident", [P, P])
        g_col, b_col, ones = mem.sbuf("g_col", [C, 1]), mem.sbuf("b_col", [C, 1]), mem.sbuf("ones", [C, 1])
        scale, shift, tmp = mem.sbuf("scale", [C, 1]), mem.sbuf("shift", [C, 1]), mem.sbuf("tmp", [C, 4])
        gap = mem.sbuf("gap", [C, CHUNKS])
        near = mem.sbuf("near", [C, 1])
        redo = mem.sbuf("redo", [1, 1], I32)
        y_last = mem.sbuf("y_last", [C, 1])
        product = [mem.psum(f"product{g}", [C, LANES]) for g in range(GROUPS)]
        turned = mem.psum("turned", [C, C])
        count = mem.psum("count", [1, 1])
        single = mem.psum("single", [C, 1])

        weights_in, ident_ready, v_turned, ready = (mem.sem(n) for n in ("weights_in", "ident", "v_turned", "ready"))
        multiplied = [mem.sem(f"multiplied{g}") for g in range(GROUPS)]
        summed = [mem.sem(f"summed{g}") for g in range(GROUPS)]
        stepped = [mem.sem(f"stepped{g}") for g in range(GROUPS)]
        halves = [{n: mem.sem(f"{n}{h}") for n in
                   ("loaded", "chain", "near", "counted", "redo_ready", "reloaded", "ready_again", "slow_product",
                    "slow_step", "stored", "kept")} for h in range(HALVES)]
        setup = 6
        per_half = WARM + CHUNK
        units_half = UNITS // HALVES

        with nc.Block() as block:
            @block.sync
            def _(sp):
                sp.dma_start(v_raw[:], V).then_inc(weights_in, 16)
                sp.dma_start(g_col[:], column(gamma)).then_inc(weights_in, 16)
                sp.dma_start(b_col[:], column(beta)).then_inc(weights_in, 16)
                for h, sems in enumerate(halves):
                    def load(done):
                        for u in range(units_half):
                            sp.dma_start(steps[:, u * UNIT:(u + 1) * UNIT], wx[h * units_half + u]).then_inc(done, 16)

                    if h:
                        sp.wait_ge(halves[h - 1]["kept"], 1)
                    load(sems["loaded"])
                    sp.wait_ge(sems["redo_ready"], 1)
                    again = sp.value_load(redo[0:1, 0:1], min_val=0, max_val=1)
                    with sp.If(again == 1):
                        load(sems["reloaded"])
                        sp.wait_ge(sems["slow_step"], HALF)
                    for u in range(units_half):
                        sp.dma_start(y_out[h * units_half + u], steps[:, u * UNIT:(u + 1) * UNIT]).then_inc(sems["stored"], 16)
                    sp.wait_ge(sems["stored"], 16 * units_half)

            @block.gpsimd
            def _(pool):
                nc.gpsimd.memset(ones[:], 1.0).then_inc(ident_ready, 1)
                nc.gpsimd.memset(ident[:], 0.0).then_inc(ident_ready, 1)
                pool.wait_ge(ident_ready, 2)
                nc.gpsimd.affine_select(out=ident[:], in_=ident[:], compare_op=ALU.not_equal, fill=1.0, base=0,
                                        pattern=[[-1, P]], channel_multiplier=1).then_inc(ident_ready, 1)
                pool.wait_ge(weights_in, 48)
                g = nc.gpsimd
                g.memset(tmp[:, 3:4], -0.5).then_inc(ready, 1)
                g.tensor_scalar(tmp[:, 0:1], wx_stats[:, 1:2], 1.0, EPS_BN, ALU.mult, ALU.add).then_inc(ready, 1)
                pool.wait_ge(ready, 2)
                g.tensor_tensor(tmp[:, 1:2], tmp[:, 0:1], tmp[:, 3:4], ALU.pow).then_inc(ready, 1)
                pool.wait_ge(ready, 3)
                g.tensor_tensor(scale[:], g_col[:], tmp[:, 1:2], ALU.mult).then_inc(ready, 1)
                pool.wait_ge(ready, 4)
                g.tensor_tensor(tmp[:, 2:3], scale[:], wx_stats[:, 0:1], ALU.mult).then_inc(ready, 1)
                pool.wait_ge(ready, 5)
                g.tensor_tensor(shift[:], b_col[:], tmp[:, 2:3], ALU.subtract).then_inc(ready, 1)

            @block.tensor
            def _(pe):
                pe.wait_ge(weights_in, 48)
                pe.wait_ge(ident_ready, 3)
                nc.tensor.transpose(turned[:], v_raw[:], ident[:]).then_inc(v_turned, 1)
                pe.wait_ge(v_turned, 2)

                def multiply(g, rhs, n):
                    pe.wait_ge(stepped[g], n)
                    nc.tensor.matmul(product[g][:], vT[:], rhs, start=True, stop=True).then_inc(multiplied[g], 1)

                for h, sems in enumerate(halves):
                    base = h * (per_half + 1)
                    for g in range(GROUPS):
                        multiply(g, warm[g][1][:], base + 1)
                    with pe.Fori(1, WARM - 1, 2) as k:
                        for odd in range(2):
                            for g in range(GROUPS):
                                multiply(g, warm[g][odd][:], k + (base + 1 + odd))
                    for g in range(GROUPS):
                        multiply(g, warm[g][0][:], base + WARM)
                    pe.wait_ge(stepped[0], base + WARM + 1)
                    for g in range(GROUPS):
                        multiply(g, first[:, g * LANES:(g + 1) * LANES], base + WARM + 1)
                    with pe.Fori(1, CHUNK) as k:
                        for g in range(GROUPS):
                            multiply(g, lanes[:, g, :, bass.ds(k - 1, 1)].rearrange("c n k -> c (n k)"), k + (base + WARM + 1))
                    pe.wait_ge(sems["near"], 1)
                    nc.tensor.matmul(count[:], near[:], ones[:], start=True, stop=True).then_inc(sems["counted"], 1)
                    pe.wait_ge(sems["redo_ready"], 1)
                    again = pe.value_load(redo[0:1, 0:1], min_val=0, max_val=1)
                    with pe.If(again == 1):
                        pe.wait_ge(sems["ready_again"], 1)
                        nc.tensor.matmul(single[:], vT[:], first[:, 0:1], start=True, stop=True).then_inc(sems["slow_product"], 1)
                        with pe.Fori(1, HALF) as t:
                            pe.wait_ge(sems["slow_step"], t)
                            nc.tensor.matmul(single[:], vT[:], steps[:, bass.ds(t - 1, 1)], start=True, stop=True
                                             ).then_inc(sems["slow_product"], 1)

            @block.vector
            def _(dve):
                dve.wait_ge(v_turned, 1)
                nc.vector.tensor_copy(vT[:], turned[:]).then_inc(v_turned, 1)
                dve.wait_ge(ready, setup)

                def add(g, part, n):
                    dve.wait_ge(multiplied[g], n)
                    nc.vector.scalar_tensor_tensor(z[g][:], part, scale[:, 0:1], product[g][:], ALU.mult, ALU.add
                                                   ).then_inc(summed[g], 1)

                for h, sems in enumerate(halves):
                    base = h * per_half
                    if h:
                        dve.wait_ge(halves[h - 1]["kept"], 1)
                    else:
                        nc.vector.memset(y_last[:], 0.0).then_inc(sems["chain"], 1)
                        dve.wait_ge(sems["chain"], 1)
                    chain = 1 if h == 0 else 0
                    nc.vector.tensor_copy(first[:, 0:1], y_last[:]).then_inc(sems["chain"], 1)
                    for g in range(GROUPS):
                        nc.vector.memset(warm[g][1][:], 0.0).then_inc(stepped[g], 1)
                    dve.wait_ge(sems["loaded"], 16 * units_half)
                    dve.wait_ge(sems["chain"], chain + 1)
                    with dve.Fori(0, WARM) as k:
                        for g in range(GROUPS):
                            add(g, lanes[:, g, :, bass.ds(k + (CHUNK - WARM), 1)].rearrange("c n k -> c (n k)"), k + (base + 1))
                    with dve.Fori(0, CHUNK) as k:
                        for g in range(GROUPS):
                            add(g, lanes[:, g, :, bass.ds(k, 1)].rearrange("c n k -> c (n k)"), k + (base + WARM + 1))
                    for g in range(GROUPS):
                        dve.wait_ge(stepped[g], (h + 1) * (per_half + 1))
                    link = sems["chain"]
                    ends = steps[:].rearrange("c (n k) -> c n k", k=CHUNK)[:, :, CHUNK - 1]
                    nc.vector.tensor_tensor(gap[:], ends, first[:, 1:CHUNKS + 1], ALU.subtract).then_inc(link, 1)
                    dve.wait_ge(link, chain + 2)
                    nc.vector.tensor_tensor(gap[:], gap[:], gap[:], ALU.mult).then_inc(link, 1)
                    dve.wait_ge(link, chain + 3)
                    nc.vector.tensor_scalar(gap[:], gap[:], TOLERANCE ** 2, None, ALU.is_le).then_inc(link, 1)
                    dve.wait_ge(link, chain + 4)
                    nc.vector.tensor_reduce(out=near[:], in_=gap[:], axis=AX.X, op=ALU.min).then_inc(sems["near"], 1)
                    dve.wait_ge(sems["counted"], 1)
                    nc.vector.tensor_scalar(redo[:], count[:], float(C) - 0.5, None, ALU.is_lt).then_inc(sems["redo_ready"], 1)
                    dve.wait_ge(sems["redo_ready"], 1)
                    again = dve.value_load(redo[0:1, 0:1], min_val=0, max_val=1)
                    with dve.If(again == 1):
                        dve.wait_ge(sems["reloaded"], 16 * units_half)
                        with dve.Fori(0, units_half) as u:
                            nc.vector.tensor_scalar(steps[:, bass.ds(u * UNIT, UNIT)], steps[:, bass.ds(u * UNIT, UNIT)],
                                                    scale[:, 0:1], shift[:, 0:1], ALU.mult, ALU.add)
                        nc.vector.tensor_copy(near[:], ones[:]).then_inc(sems["ready_again"], 1)
                        dve.wait_ge(sems["slow_step"], HALF)
                    nc.vector.tensor_copy(y_last[:], steps[:, HALF - 1:HALF]).then_inc(sems["kept"], 1)

            @block.scalar
            def _(act):
                act.wait_ge(ready, setup)

                def state(g, out, n):
                    act.wait_ge(summed[g], n)
                    nc.scalar.activation(out, z[g][:], ACT.Sigmoid, bias=shift[:, 0:1]).then_inc(stepped[g], 1)

                for h, sems in enumerate(halves):
                    base = h * per_half
                    with act.Fori(0, WARM - 2, 2) as k:
                        for odd in range(2):
                            for g in range(GROUPS):
                                state(g, warm[g][odd][:], k + (base + 1 + odd))
                    for g in range(GROUPS):
                        state(g, warm[g][0][:], base + WARM - 1)
                    for g in range(GROUPS):
                        state(g, first[:, g * LANES + 1:(g + 1) * LANES + 1], base + WARM)
                    with act.Fori(0, CHUNK) as k:
                        for g in range(GROUPS):
                            state(g, lanes[:, g, :, bass.ds(k, 1)].rearrange("c n k -> c (n k)"), k + (base + WARM + 1))
                    act.wait_ge(sems["redo_ready"], 1)
                    again = act.value_load(redo[0:1, 0:1], min_val=0, max_val=1)
                    with act.If(again == 1):
                        act.wait_ge(sems["ready_again"], 1)
                        with act.Fori(0, HALF) as t:
                            act.wait_ge(sems["slow_product"], t + 1)
                            nc.scalar.activation(steps[:, bass.ds(t, 1)], single[:], ACT.Sigmoid,
                                                 bias=steps[:, bass.ds(t, 1)]).then_inc(sems["slow_step"], 1)

        mem.clear()


def gates(nc, x1, y, norm_g, norm_b, weights, biases, x2, left, right, out_gate):
    with ExitStack() as stack:
        mem = Memory(nc, stack, "gates")
        norm = RowNorm(mem, 1 + EPS_LN, EPS_C * EPS_LN)
        x_in = [mem.sbuf(f"x{s}", [P, TILES, C]) for s in range(AHEAD)]
        y_in = [mem.sbuf(f"y{s}", [C, UNIT]) for s in range(AHEAD)]
        x2_sb = [mem.sbuf(f"x2{s}", [P, TILES, C]) for s in range(AHEAD)]
        centred = [mem.sbuf(f"centred{s}", [P, TILES, C]) for s in range(2)]
        xT = [mem.sbuf(f"xT{s}", [C, UNIT]) for s in range(2)]
        xT_parts = [[mem.sbuf(f"xT_{part}{s}", [C, UNIT], F32R) for part in ("high", "low")] for s in range(2)]
        w_parts = [[mem.sbuf(f"w_{part}{n}", [C, C], F32R) for part in ("high", "low")] for n in range(5)]
        sides = [[mem.sbuf(f"side{n}{s}", [C, UNIT]) for s in range(2)] for n in range(2)]
        gate = [mem.sbuf(f"gate{s}", [C, BANK]) for s in range(2)]
        og = [mem.sbuf(f"og{s}", [C, UNIT]) for s in range(2)]
        w = [mem.sbuf(f"w{n}", [C, C]) for n in range(5)]
        b = [mem.sbuf(f"b{n}", [C, 1]) for n in range(5)]
        g_col, b_col, ident = mem.sbuf("g_col", [C, 1]), mem.sbuf("b_col", [C, 1]), mem.sbuf("ident", [P, P])
        y_turned = mem.psum("y_turned", [P, TILES, C])
        turned = mem.psum("turned", [C, UNIT])
        gate_bank = [mem.psum(f"gate_bank{n}", [C, BANK]) for n in range(2)]
        side_bank = [mem.psum(f"side_bank{n}", [C, BANK]) for n in range(2)]

        weights_in, ident_ready = mem.sem("weights_in"), mem.sem("ident")
        x_loaded, y_loaded = mem.sems("x_loaded", AHEAD), mem.sems("y_loaded", AHEAD)
        x2_stored, left_stored, right_stored, og_stored = mem.sems("x2_stored", AHEAD), mem.sems("left_stored"), mem.sems("right_stored"), mem.sems("og_stored")
        (y_turned_ready, x2_ready, stats_ready, rstd_ready, centred_ready, turned_ready, xT_ready, high_part, parts_ready, w_split, gate_product,
         side_product, gate_ready, side_ready) = (mem.sem(n) for n in (
             "y_turned_ready", "x2_ready", "stats", "rstd", "centred_ready", "turned_ready", "xT_ready", "high_part", "parts_ready",
             "w_split", "gate_product",
             "side_product", "gate_ready", "side_ready"))
        loads = 16 * 12
        GATES_A_UNIT, SIDES_A_UNIT = 6, 4
        x_units = x1.rearrange("(u t p) c -> u p t c", t=TILES, p=P)
        x2_units = x2.rearrange("(u t p) c -> u p t c", t=TILES, p=P)

        with nc.Block() as block:
            @block.sync
            def _(sp):
                for n in range(5):
                    sp.dma_start(w[n][:], weights[n]).then_inc(weights_in, 16)
                    sp.dma_start(b[n][:], column(biases[n])).then_inc(weights_in, 16)
                sp.dma_start(g_col[:], column(norm_g)).then_inc(weights_in, 16)
                sp.dma_start(b_col[:], column(norm_b)).then_inc(weights_in, 16)

                def step(u, s):
                    wait_unit(sp, x2_ready, u - AHEAD)
                    sp.dma_start(x_in[s][:], x_units[u]).then_inc(x_loaded[s], 16)
                    sp.dma_start(y_in[s][:], y[u]).then_inc(y_loaded[s], 16)
                    if exists(u - AHEAD, UNITS):
                        store(u - AHEAD, s)

                def store(u, s):
                    wait_unit(sp, x2_ready, u)
                    sp.dma_start(x2_units[u], x2_sb[s][:]).then_inc(x2_stored[s], 16)
                    wait_unit(sp, side_ready, u, per=SIDES_A_UNIT)
                    wait_unit(sp, gate_ready, u, per=GATES_A_UNIT)
                    cols = bass.ds(u * UNIT, UNIT)
                    sp.dma_start(left[:, cols], sides[0][s % 2][:]).then_inc(left_stored[s % 2], 16)
                    sp.dma_start(right[:, cols], sides[1][s % 2][:]).then_inc(right_stored[s % 2], 16)
                    sp.dma_start(out_gate[u], og[s % 2][:]).then_inc(og_stored[s % 2], 16)

                each_unit(sp, UNITS, AHEAD, step)
                for s in range(AHEAD):
                    store(UNITS - AHEAD + s, s)
                for s in range(2):
                    for sems in (left_stored, right_stored, og_stored):
                        wait_dma(sp, sems, UNITS - 2 + s, s)
                for s in range(AHEAD):
                    wait_dma(sp, x2_stored, UNITS - AHEAD + s, s, AHEAD)

            @block.tensor
            def _(pe):
                pe.wait_ge(ident_ready, 2)
                pe.wait_ge(weights_in, loads)
                pe.wait_ge(w_split, 2)

                def turn_y(u, s):
                    wait_dma(pe, y_loaded, u, s % AHEAD, AHEAD)
                    wait_unit(pe, x2_ready, u - 1)
                    for t in range(TILES):
                        last = nc.tensor.transpose(y_turned[:, t, :], y_in[s % AHEAD][:, t * P:(t + 1) * P], ident[:])
                    last.then_inc(y_turned_ready, 1)

                def project(u, s):
                    wait_unit(pe, parts_ready, u)
                    for half in range(2):
                        rhs = [part[:, half * BANK:(half + 1) * BANK] for part in xT_parts[s % 2]]
                        for n in range(5):
                            if n in (1, 3):
                                k = 2 * half + (n == 3)
                                wait_count(pe, side_ready, u * SIDES_A_UNIT + (k - 1))
                                split_matmul(nc, side_bank[k % 2][:], [part[:] for part in w_parts[n]], rhs
                                             ).then_inc(side_product, 1)
                            else:
                                k = 3 * half + n // 2
                                wait_count(pe, gate_ready, u * GATES_A_UNIT + (k - 1))
                                split_matmul(nc, gate_bank[k % 2][:], [part[:] for part in w_parts[n]], rhs
                                             ).then_inc(gate_product, 1)

                turn_y(0, 0)
                turn_y(1, 1)
                turn_y(2, 2)

                def step(u, s):
                    wait_unit(pe, centred_ready, u, per=2)
                    wait_unit(pe, xT_ready, u - 1)
                    for t in range(TILES):
                        last = nc.tensor.transpose(turned[:, t * P:(t + 1) * P], centred[s % 2][:, t, :], ident[:])
                    last.then_inc(turned_ready, 1)
                    if exists(u - 1, UNITS):
                        project(u - 1, s - 1)
                    if exists(u + 3, UNITS):
                        turn_y(u + 3, s + 3)

                each_unit(pe, UNITS, AHEAD, step)
                project(UNITS - 1, UNITS - 1)

            @block.vector
            def _(dve):
                def add_y(u, s):
                    wait_dma(dve, x_loaded, u, s % AHEAD, AHEAD)
                    wait_unit(dve, y_turned_ready, u)
                    wait_unit(dve, centred_ready, u - AHEAD, per=2)
                    wait_dma(dve, x2_stored, u - AHEAD, s % AHEAD, AHEAD)
                    nc.vector.tensor_tensor(x2_sb[s % AHEAD][:].rearrange("p t c -> p (t c)"),
                                            y_turned[:].rearrange("p t c -> p (t c)"),
                                            x_in[s % AHEAD][:].rearrange("p t c -> p (t c)"), ALU.add).then_inc(x2_ready, 1)

                def stats(u, s):
                    wait_unit(dve, x2_ready, u)
                    wait_unit(dve, rstd_ready, u - 2)
                    tile_stats(nc, norm.stats[s % 2], x2_sb[s % AHEAD], stats_ready)

                def centre(u, s, half):
                    wait_unit(dve, rstd_ready, u)
                    wait_unit(dve, turned_ready, u - 2)
                    norm.apply(nc, s % 2, centred[s % 2], x2_sb[s % AHEAD], centred_ready,
                               range(half * TILES // 2, (half + 1) * TILES // 2))

                def multiply(u, s, k):
                    half, n = k // 2, k % 2
                    if half == 0:
                        wait_dma(dve, (left_stored, right_stored)[n], u - 2, s % 2)
                    wait_count(dve, side_product, u * SIDES_A_UNIT + (k + 1))
                    wait_count(dve, gate_ready, u * GATES_A_UNIT + (3 * half + n + 1))
                    nc.vector.scalar_tensor_tensor(sides[n][s % 2][:, half * BANK:(half + 1) * BANK],
                                                   side_bank[k % 2][:], b[2 * n + 1][:, 0:1], gate[n][:],
                                                   ALU.add, ALU.mult).then_inc(side_ready, 1)

                dve.wait_ge(weights_in, loads)
                for n in range(5):
                    last = nc.vector.tensor_copy(w_parts[n][0][:], w[n][:])
                last.then_inc(w_split, 1)
                dve.wait_ge(w_split, 1)
                for n in range(5):
                    last = nc.vector.tensor_tensor(w_parts[n][1][:], w[n][:], w_parts[n][0][:], ALU.subtract)
                last.then_inc(w_split, 1)
                for u in range(2):
                    add_y(u, u)
                    stats(u, u)
                for half in range(2):
                    centre(0, 0, half)

                def step(u, s):
                    before, after = exists(u - 1, UNITS), exists(u + 1, UNITS)
                    if before:
                        multiply(u - 1, s + 1, 0)
                    if exists(u + 2, UNITS):
                        add_y(u + 2, s + 2)
                    if before:
                        multiply(u - 1, s + 1, 1)
                    if after:
                        centre(u + 1, s + 1, 0)
                    if before:
                        multiply(u - 1, s + 1, 2)
                    if after:
                        centre(u + 1, s + 1, 1)
                    if before:
                        multiply(u - 1, s + 1, 3)
                    if exists(u + 2, UNITS):
                        stats(u + 2, s + 2)

                each_unit(dve, UNITS, AHEAD, step)
                for k in range(SIDES_A_UNIT):
                    multiply(UNITS - 1, UNITS - 1, k)

            @block.gpsimd
            def _(pool):
                make_identity(nc, ident, ident_ready)
                norm.prepare(nc)

                def norms(u, s):
                    wait_unit(pool, stats_ready, u)
                    wait_unit(pool, centred_ready, u - 2, per=2)
                    norm.rstd_of(nc, u, s % 2, rstd_ready)

                norms(0, 0)
                norms(1, 1)

                def step(u, s):
                    wait_unit(pool, high_part, u, per=2)
                    wait_unit(pool, gate_product, u - 2, per=GATES_A_UNIT)
                    nc.gpsimd.tensor_tensor(xT_parts[s % 2][1][:], xT[s % 2][:], xT_parts[s % 2][0][:], ALU.subtract
                                            ).then_inc(parts_ready, 1)
                    if exists(u + 2, UNITS):
                        norms(u + 2, s)

                each_unit(pool, UNITS, 2, step)

            @block.scalar
            def _(act):
                act.wait_ge(weights_in, loads)

                def take_gates(u, s, products):
                    for k in products:
                        half, n = k // 3, k % 3
                        wait_count(act, gate_product, u * GATES_A_UNIT + (k + 1))
                        if n < 2:
                            wait_count(act, side_ready, u * SIDES_A_UNIT + (2 * half + n - 1))
                            out = gate[n][:]
                        else:
                            if half == 0:
                                wait_dma(act, og_stored, u - 2, s % 2)
                            out = og[s % 2][:, half * BANK:(half + 1) * BANK]
                        nc.scalar.activation(out, gate_bank[k % 2][:], ACT.Sigmoid, bias=b[2 * n][:, 0:1]
                                             ).then_inc(gate_ready, 1)

                def take_turned(u, s):
                    wait_unit(act, turned_ready, u)
                    wait_unit(act, parts_ready, u - 2)
                    for half in range(2):
                        cols = slice(half * BANK, (half + 1) * BANK)
                        last = nc.scalar.activation(xT[s % 2][:, cols], turned[:, cols], ACT.Identity,
                                                    scale=g_col[:, 0:1], bias=b_col[:, 0:1])
                    last.then_inc(xT_ready, 1)

                def take_high(u, s, half):
                    wait_unit(act, xT_ready, u)
                    wait_unit(act, gate_product, u - 2, per=GATES_A_UNIT)
                    cols = slice(half * BANK, (half + 1) * BANK)
                    nc.scalar.copy(xT_parts[s % 2][0][:, cols], xT[s % 2][:, cols]).then_inc(high_part, 1)

                def step(u, s):
                    before = exists(u - 1, UNITS)
                    take_turned(u, s)
                    if before:
                        take_gates(u - 1, s + 1, range(0, 2))
                    take_high(u, s, 0)
                    if before:
                        take_gates(u - 1, s + 1, range(2, 3))
                    take_high(u, s, 1)
                    if before:
                        take_gates(u - 1, s + 1, range(3, 6))

                each_unit(act, UNITS, AHEAD, step)
                take_gates(UNITS - 1, UNITS - 1, range(GATES_A_UNIT))

        mem.clear()


def triangle(nc, left, right, out):
    with ExitStack() as stack:
        mem = Memory(nc, stack, "tri")
        l = [mem.sbuf(f"l{s}", [P, 2, COLS]) for s in range(AHEAD)]
        r = [mem.sbuf(f"r{s}", [P, 2, COLS]) for s in range(AHEAD)]
        o = [mem.sbuf(f"o{s}", [P, 2, COLS]) for s in range(AHEAD)]
        product = [mem.psum(f"product{s}", [P, 2, COLS]) for s in range(AHEAD)]
        l_loaded, r_loaded, stored = mem.sems("l_loaded", AHEAD), mem.sems("r_loaded", AHEAD), mem.sems("stored", AHEAD)
        multiplied, o_ready = mem.sem("multiplied"), mem.sem("o_ready")

        def channel(t, d):
            return t[bass.ds(d, 1), 0:TOKENS].rearrange("a (k p j) -> p (a k) j", k=2, p=P)

        with nc.Block() as block:
            @block.sync
            def _(sp):
                def step(d, s):
                    wait_unit(sp, multiplied, d - AHEAD)
                    sp.dma_start(l[s][:], channel(left, d)).then_inc(l_loaded[s], 16)
                    sp.dma_start(r[s][:], channel(right, d)).then_inc(r_loaded[s], 16)

                each_unit(sp, C, AHEAD, step)

            @block.tensor
            def _(pe):
                def step(d, s):
                    wait_dma(pe, l_loaded, d, s, AHEAD)
                    wait_dma(pe, r_loaded, d, s, AHEAD)
                    wait_unit(pe, o_ready, d - AHEAD)
                    for i in range(2):
                        for k in range(2):
                            last = nc.tensor.matmul(product[s][:, i, :], r[s][:, k, i * P:(i + 1) * P], l[s][:, k, :],
                                                    start=(k == 0), stop=(k == 1))
                    last.then_inc(multiplied, 1)

                each_unit(pe, C, AHEAD, step)

            @block.vector
            def _(dve):
                def step(d, s):
                    wait_unit(dve, multiplied, d)
                    wait_dma(dve, stored, d - AHEAD, s, AHEAD)
                    nc.vector.tensor_copy(o[s][:], product[s][:]).then_inc(o_ready, 1)

                each_unit(dve, C, AHEAD, step)

            @block.scalar
            def _(act):
                def step(d, s):
                    wait_unit(act, o_ready, d)
                    act.dma_start(channel(out, d), o[s][:]).then_inc(stored[s], 16)

                each_unit(act, C, AHEAD, step)
                for s in range(AHEAD):
                    wait_dma(act, stored, C - AHEAD + s, s, AHEAD)

        mem.clear()


def triangle_out(nc, tri, out_gate, x2, norm_g, norm_b, w_out, b_out, x3):
    with ExitStack() as stack:
        mem = Memory(nc, stack, "out")
        norm = RowNorm(mem, 1.0, EPS_LN, for_scalar=True)
        tri_in = [mem.sbuf(f"tri{s}", [C, UNIT]) for s in range(AHEAD)]
        og = [mem.sbuf(f"og{s}", [C, UNIT]) for s in range(AHEAD)]
        x_in = [mem.sbuf(f"x{s}", [P, TILES, C]) for s in range(AHEAD)]
        centred = [mem.sbuf(f"centred{s}", [P, TILES, C]) for s in range(2)]
        normed = [mem.sbuf(f"normed{s}", [C, UNIT]) for s in range(2)]
        gated = [mem.sbuf(f"gated{s}", [C, UNIT]) for s in range(2)]
        x_b = [mem.sbuf(f"x_b{s}", [P, TILES, C]) for s in range(2)]
        x3_sb = [mem.sbuf(f"x3{s}", [P, TILES, C]) for s in range(2)]
        w, b_all, ident = mem.sbuf("w", [C, C]), mem.sbuf("b_all", [P, C]), mem.sbuf("ident", [P, P])
        g_col, b_col = mem.sbuf("g_col", [C, 1]), mem.sbuf("b_col", [C, 1])
        tokens = [mem.psum(f"tokens{s}", [P, TILES, C]) for s in range(2)]
        turned = mem.psum("turned", [C, UNIT])
        product = mem.psum("product", [P, TILES, C])

        weights_in, ident_ready = mem.sem("weights_in"), mem.sem("ident")
        tri_loaded, og_loaded, x_loaded = mem.sems("tri_loaded", AHEAD), mem.sems("og_loaded", AHEAD), mem.sems("x_loaded", AHEAD)
        stored = mem.sems("stored")
        (tokens_ready, stats_ready, rstd_ready, centred_ready, turned_ready, normed_ready, gated_ready, product_ready,
         x_b_ready, x3_ready) = (mem.sem(n) for n in ("tokens_ready", "stats", "rstd", "centred_ready", "turned_ready",
                                                      "normed_ready", "gated_ready", "product_ready", "x_b_ready", "x3_ready"))
        loads = 16 * 4
        x_units = x2.rearrange("(u t p) c -> u p t c", t=TILES, p=P)
        x3_units = x3.rearrange("(u t p) c -> u p t c", t=TILES, p=P)

        with nc.Block() as block:
            @block.sync
            def _(sp):
                sp.dma_start(w[:], w_out).then_inc(weights_in, 16)
                sp.dma_start(b_all[:], row_to_all(b_out)).then_inc(weights_in, 16)
                sp.dma_start(g_col[:], column(norm_g)).then_inc(weights_in, 16)
                sp.dma_start(b_col[:], column(norm_b)).then_inc(weights_in, 16)

                def step(u, s):
                    wait_unit(sp, tokens_ready, u - AHEAD)
                    sp.dma_start(tri_in[s][:], tri[:, bass.ds(u * UNIT, UNIT)]).then_inc(tri_loaded[s], 16)
                    wait_unit(sp, x_b_ready, u - AHEAD)
                    sp.dma_start(x_in[s][:], x_units[u]).then_inc(x_loaded[s], 16)
                    wait_unit(sp, gated_ready, u - AHEAD)
                    sp.dma_start(og[s][:], out_gate[u]).then_inc(og_loaded[s], 16)

                each_unit(sp, UNITS, AHEAD, step)

            @block.tensor
            def _(pe):
                pe.wait_ge(ident_ready, 2)
                pe.wait_ge(weights_in, loads)

                def to_tokens(u, s):
                    wait_dma(pe, tri_loaded, u, s % AHEAD, AHEAD)
                    wait_unit(pe, centred_ready, u - 2)
                    for t in range(TILES):
                        last = nc.tensor.transpose(tokens[s % 2][:, t, :], tri_in[s % AHEAD][:, t * P:(t + 1) * P], ident[:])
                    last.then_inc(tokens_ready, 1)

                def project(u, s):
                    wait_unit(pe, gated_ready, u)
                    wait_unit(pe, x3_ready, u - 1)
                    for t in range(TILES):
                        last = nc.tensor.matmul(product[:, t, :], gated[s % 2][:, t * P:(t + 1) * P], w[:], start=True, stop=True)
                    last.then_inc(product_ready, 1)

                to_tokens(0, 0)
                to_tokens(1, 1)

                def step(u, s):
                    if exists(u + 2, UNITS):
                        to_tokens(u + 2, s + 2)
                    wait_unit(pe, centred_ready, u)
                    wait_unit(pe, normed_ready, u - 1)
                    for t in range(TILES):
                        last = nc.tensor.transpose(turned[:, t * P:(t + 1) * P], centred[s % 2][:, t, :], ident[:])
                    last.then_inc(turned_ready, 1)
                    if exists(u - 1, UNITS):
                        project(u - 1, s + 1)

                each_unit(pe, UNITS, AHEAD, step)
                project(UNITS - 1, UNITS - 1)

            @block.vector
            def _(dve):
                def stats(u, s):
                    wait_unit(dve, tokens_ready, u)
                    wait_unit(dve, rstd_ready, u - 2)
                    tile_stats(nc, norm.stats[s % 2], tokens[s % 2], stats_ready)

                def finish(u, s):
                    wait_unit(dve, product_ready, u)
                    wait_unit(dve, x_b_ready, u)
                    wait_dma(dve, stored, u - 2, s % 2)
                    nc.vector.tensor_tensor(x3_sb[s % 2][:].rearrange("p t c -> p (t c)"),
                                            product[:].rearrange("p t c -> p (t c)"),
                                            x_b[s % 2][:].rearrange("p t c -> p (t c)"), ALU.add).then_inc(x3_ready, 1)

                def gating(u, s):
                    wait_unit(dve, normed_ready, u)
                    wait_dma(dve, og_loaded, u, s % AHEAD, AHEAD)
                    wait_unit(dve, product_ready, u - 2)
                    nc.vector.tensor_tensor(gated[s % 2][:], normed[s % 2][:], og[s % AHEAD][:], ALU.mult).then_inc(gated_ready, 1)

                stats(0, 0)
                stats(1, 1)

                def step(u, s):
                    if exists(u + 2, UNITS):
                        stats(u + 2, s)
                    if exists(u - 1, UNITS):
                        finish(u - 1, s + 3)
                    gating(u, s)

                each_unit(dve, UNITS, AHEAD, step)
                finish(UNITS - 1, UNITS - 1)

            @block.gpsimd
            def _(pool):
                make_identity(nc, ident, ident_ready)
                norm.prepare(nc)
                pool.wait_ge(weights_in, loads)

                def norms(u, s):
                    wait_unit(pool, stats_ready, u)
                    wait_unit(pool, centred_ready, u - 2)
                    norm.rstd_of(nc, u, s % 2, rstd_ready)

                norms(0, 0)
                norms(1, 1)

                def step(u, s):
                    if exists(u + 2, UNITS):
                        norms(u + 2, s)
                    wait_dma(pool, x_loaded, u, s, AHEAD)
                    wait_unit(pool, x3_ready, u - 2)
                    nc.gpsimd.tensor_tensor(x_b[s % 2][:], x_in[s][:], b_all[:].unsqueeze(1).to_broadcast([P, TILES, C]),
                                            ALU.add).then_inc(x_b_ready, 1)

                each_unit(pool, UNITS, AHEAD, step)

            @block.scalar
            def _(act):
                act.wait_ge(weights_in, loads)

                def store(u, s):
                    wait_unit(act, x3_ready, u)
                    act.dma_start(x3_units[u], x3_sb[s % 2][:]).then_inc(stored[s % 2], 16)

                def centre(u, s):
                    wait_unit(act, rstd_ready, u)
                    wait_unit(act, turned_ready, u - 2)
                    norm.apply_on_scalar(nc, s % 2, centred[s % 2], tokens[s % 2], centred_ready)

                centre(0, 0)

                def step(u, s):
                    if exists(u + 1, UNITS):
                        centre(u + 1, s + 1)
                    wait_unit(act, turned_ready, u)
                    wait_unit(act, gated_ready, u - 2)
                    for half in range(2):
                        cols = slice(half * BANK, (half + 1) * BANK)
                        last = nc.scalar.activation(normed[s % 2][:, cols], turned[:, cols], ACT.Identity,
                                                    scale=g_col[:, 0:1], bias=b_col[:, 0:1])
                    last.then_inc(normed_ready, 1)
                    if exists(u - 2, UNITS):
                        store(u - 2, s)

                each_unit(act, UNITS, AHEAD, step)
                for u in (UNITS - 2, UNITS - 1):
                    store(u, u)
                for s in range(2):
                    wait_dma(act, stored, UNITS - 2 + s, s)

        mem.clear()


SHARED = (0, 2, 4, 5, 7)


def adding_order():
    timed = []
    for t in range(TILES):
        if t in SHARED:
            timed += [(4 * t + 2 * e, t, e) for e in range(EXPERTS // 2)]
        else:
            timed += [(4 * t + e, t, e) for e in range(EXPERTS)]
    timed.sort()
    return [[(t, e) for time, t, e in timed if min(time // 4, TILES - 1) == part] for part in range(TILES)]


def experts(nc, x3, router_w, router_b, expert_w, expert_b, x4):
    E, HALF_E = EXPERTS, EXPERTS // 2
    with ExitStack() as stack:
        mem = Memory(nc, stack, "moe")
        norm = RowNorm(mem, 1.0, EPS_T, for_scalar=True)
        x_in = [mem.sbuf(f"x{s}", [P, TILES, C]) for s in range(AHEAD)]
        centred = [mem.sbuf(f"centred{s}", [P, TILES, C]) for s in range(2)]
        xT = [mem.sbuf(f"xT{s}", [C, UNIT]) for s in range(2)]
        xT_parts = [[mem.sbuf(f"xT_{part}{s}", [C, UNIT], F32R) for part in ("high", "low")] for s in range(2)]
        w_all = mem.sbuf("w_all", [C, E * C])
        w_parts = [mem.sbuf(f"w_{part}", [C, E * C], F32R) for part in ("high", "low")]
        w_router = mem.sbuf("w_router", [C, E])
        b_router = mem.sbuf("b_router", [P, E])
        b_blocks = mem.sbuf("b_blocks", [TILES * E, TILES, C])
        ident = mem.sbuf("ident", [P, P])
        logits = mem.sbuf("logits", [P, TILES, E])
        best = mem.sbuf("best", [P, TILES, 8])
        shifted, chosen, equal, share, unscaled = (mem.sbuf(n, [P, TILES, E]) for n in (
            "shifted", "chosen", "equal", "share", "unscaled"))
        rank = [mem.sbuf(f"rank{n}", [P, TILES, E]) for n in range(3)]
        first = mem.sbuf("first", [P, TILES, E])
        wait_tick = mem.sbuf("wait_tick", [P, 2])
        alike, places, ones = (mem.sbuf(n, [P, TILES]) for n in ("alike", "places", "ones"))
        total, inv = mem.sbuf("total", [P, TILES]), mem.sbuf("inv", [P, TILES])
        weight = [mem.sbuf(f"weight{s}", [P, TILES, E]) for s in range(2)]
        weightT_parts = [mem.sbuf(f"weightT_{part}", [TILES * E, P], F32R) for part in ("high", "low")]
        b_parts = [mem.sbuf(f"b_{part}", [TILES * E, TILES, C], F32R) for part in ("high", "low")]
        acc = [mem.sbuf(f"acc{s}", [P, TILES, C]) for s in range(2)]
        upper = [mem.sbuf(f"upper{n}", [P, HALF_E, C]) for n in range(len(SHARED))]
        pairs = [mem.sbuf(f"pairs{n}", [P, 2, C]) for n in range(len(SHARED))]
        upper_sum = [mem.sbuf(f"upper_sum{n}", [P, C]) for n in range(len(SHARED))]
        out = [mem.sbuf(f"out{s}", [P, TILES, C]) for s in range(2)]
        turned = mem.psum("turned", [C, UNIT])
        small = mem.psum("small", [P, TILES * E])
        small_turned = mem.psum("small_turned", [TILES * E, P])
        low = [mem.psum(f"low{n}", [P, HALF_E * C]) for n in range(2)]
        high = [mem.psum(f"high{n}", [P, HALF_E * C]) for n in range(2)]

        weights_in, ident_ready, blocks_zero = mem.sem("weights_in"), mem.sem("ident"), mem.sem("blocks_zero")
        x_loaded, stored = mem.sems("x_loaded", AHEAD), mem.sems("stored")
        (stats_ready, rstd_ready, centred_ready, turned_ready, xT_ready, high_part, parts_ready, w_split, logits_product, logits_ready, best_ready,
         exp_ready, route_step, total_ready, inv_ready, shifted_ready, compared, chosen_ready, unscaled_ready, weight_ready, weight_turned,
         weightT_ready, bias_product, acc_ready, low_product, high_product, added, scaled, upper_step,
         upper_summed) = (
            mem.sem(n) for n in ("stats", "rstd", "centred_ready", "turned_ready", "xT_ready", "high_part",
                                 "parts_ready", "w_split", "logits_product",
                                 "logits_ready", "best_ready", "exp_ready", "route_step", "total_ready", "inv_ready",
                                 "shifted_ready", "compared", "chosen_ready", "unscaled_ready", "weight_ready", "weight_turned", "weightT_ready",
                                 "bias_product", "acc_ready", "low_product", "high_product", "added", "scaled",
                                 "upper_step", "upper_summed"))
        ROUTE = 6
        order = adding_order()
        place = {item: n for n, item in enumerate(item for part in order for item in part)}
        ADDED, SCALED = len(place), len(SHARED)

        def wait_added(eng, u, t, e):
            wait_count(eng, added, u * ADDED + (place[t % TILES, e] + 1 - (ADDED if t < 0 else 0)))

        def wait_scaled(eng, u, t):
            wait_count(eng, scaled, u * SCALED + (SHARED.index(t % TILES) + 1 - (SCALED if t < 0 else 0)))

        loads = 16 * (E + 2 + TILES)
        x_units = x3.rearrange("(u t p) c -> u p t c", t=TILES, p=P)
        x4_units = x4.rearrange("(u t p) c -> u p t c", t=TILES, p=P)

        with nc.Block() as block:
            @block.sync
            def _(sp):
                for e in range(E):
                    sp.dma_start(w_all[:, e * C:(e + 1) * C], expert_w[e]).then_inc(weights_in, 16)
                sp.dma_start(w_router[:], router_w).then_inc(weights_in, 16)
                sp.dma_start(b_router[:], row_to_all(router_b)).then_inc(weights_in, 16)
                sp.wait_ge(blocks_zero, 1)
                for t in range(TILES):
                    sp.dma_start(b_blocks[t * E:(t + 1) * E, t, :], expert_b).then_inc(weights_in, 16)

                def step(u, s):
                    wait_unit(sp, acc_ready, u - AHEAD)
                    sp.dma_start(x_in[s][:], x_units[u]).then_inc(x_loaded[s], 16)

                each_unit(sp, UNITS, AHEAD, step)

            @block.tensor
            def _(pe):
                pe.wait_ge(ident_ready, 2)
                pe.wait_ge(weights_in, loads)

                def turn(u, s):
                    wait_unit(pe, centred_ready, u, per=2)
                    wait_unit(pe, acc_ready, u - 1)
                    for t in range(TILES):
                        last = nc.tensor.transpose(turned[:, t * P:(t + 1) * P], centred[s % 2][:, t, :], ident[:])
                    last.then_inc(turned_ready, 1)

                def route(u, s):
                    wait_unit(pe, xT_ready, u)
                    wait_unit(pe, logits_ready, u - 1)
                    for t in range(TILES):
                        last = nc.tensor.matmul(small[:, t * E:(t + 1) * E], xT[s % 2][:, t * P:(t + 1) * P], w_router[:],
                                                start=True, stop=True)
                    last.then_inc(logits_product, 1)

                def turn_weights(u, s):
                    wait_alone(pe, weight_ready, u + 1, weights_in, loads)
                    nc.tensor.transpose(small_turned[:], weight[s % 2][:].rearrange("p t e -> p (t e)"), ident[:]
                                        ).then_inc(weight_turned, 1)

                def biases(u, s):
                    wait_unit(pe, weightT_ready, u, per=2)
                    wait_unit(pe, high_part, u)
                    for half in range(2):
                        last = split_matmul(nc, turned[:, half * BANK:(half + 1) * BANK], [w[:] for w in weightT_parts],
                                            [b[:, half * 4:(half + 1) * 4, :].rearrange("r t c -> r (t c)") for b in b_parts])
                    last.then_inc(bias_product, 1)

                def multiply(u, s, tiles):
                    for t in tiles:
                        if t == 0:
                            wait_unit(pe, parts_ready, u)
                        lhs = [part[:, t * P:(t + 1) * P] for part in xT_parts[s % 2]]
                        wait_added(pe, u, t - 2, HALF_E - 1)
                        split_matmul(nc, low[t % 2][:], lhs, [part[:, 0:BANK] for part in w_parts]).then_inc(low_product, 1)
                        if (t - 2) % TILES in SHARED:
                            wait_scaled(pe, u, t - 2)
                        else:
                            wait_added(pe, u, t - 2, E - 1)
                        split_matmul(nc, high[t % 2][:], lhs, [part[:, BANK:2 * BANK] for part in w_parts]
                                     ).then_inc(high_product, 1)

                pe.wait_ge(w_split, 2)
                turn(0, 0)
                route(0, 0)
                turn_weights(0, 0)
                biases(0, 0)

                def step(u, s):
                    multiply(u, s, range(0, 1))
                    if exists(u + 1, UNITS):
                        turn(u + 1, s + 1)
                    multiply(u, s, range(1, 2))
                    if exists(u + 1, UNITS):
                        route(u + 1, s + 1)
                    multiply(u, s, range(2, 5))
                    if exists(u + 1, UNITS):
                        turn_weights(u + 1, s + 1)
                    multiply(u, s, range(5, 8))
                    if exists(u + 1, UNITS):
                        biases(u + 1, s + 1)

                each_unit(pe, UNITS, AHEAD, step)

            @block.vector
            def _(dve):
                dve.wait_ge(weights_in, loads)
                nc.vector.tensor_copy(w_parts[0][:], w_all[:])
                nc.vector.tensor_copy(b_parts[0][:], b_blocks[:]).then_inc(w_split, 1)
                dve.wait_ge(w_split, 1)
                nc.vector.tensor_tensor(b_parts[1][:], b_blocks[:], b_parts[0][:], ALU.subtract)
                nc.vector.tensor_tensor(w_parts[1][:], w_all[:], w_parts[0][:], ALU.subtract).then_inc(w_split, 1)

                def stats(u, s, half):
                    wait_dma(dve, x_loaded, u, s % AHEAD, AHEAD)
                    wait_unit(dve, rstd_ready, u - 2)
                    for t in range(half * TILES // 2, (half + 1) * TILES // 2):
                        last = nc.vector.bn_stats(norm.stats[s % 2][:, t, :], x_in[s % AHEAD][:, t, :])
                    last.then_inc(stats_ready, 1)

                def route(u, s):
                    wait_unit(dve, logits_product, u)
                    nc.vector.tensor_tensor(logits[:], small[:].rearrange("p (t e) -> p t e", e=E),
                                            b_router[:].unsqueeze(1).to_broadcast([P, TILES, E]), ALU.add
                                            ).then_inc(logits_ready, 1)
                    wait_alone(dve, logits_ready, u + 1, weights_in, loads)
                    for t in range(TILES):
                        last = nc.vector.max(out=best[:, t, :], in_=logits[:, t, :])
                    last.then_inc(best_ready, 1)

                def compare(u, s):
                    wait_unit(dve, best_ready, u)
                    nc.vector.tensor_tensor(shifted[:], logits[:], best[:, :, 0:1].to_broadcast([P, TILES, E]), ALU.subtract
                                            ).then_inc(shifted_ready, 1)
                    second = best[:, :, 1:2].to_broadcast([P, TILES, E])
                    nc.vector.tensor_tensor(equal[:], logits[:], second, ALU.is_equal)
                    nc.vector.tensor_tensor(first[:], logits[:], second, ALU.is_gt)
                    nc.vector.tensor_tensor(alike[:], best[:, :, 0], best[:, :, 1], ALU.is_equal).then_inc(compared, 1)

                def finish_weights(u, s):
                    wait_unit(dve, chosen_ready, u)
                    wait_unit(dve, exp_ready, u)
                    nc.vector.tensor_tensor(unscaled[:], share[:], chosen[:], ALU.mult).then_inc(unscaled_ready, 1)
                    wait_unit(dve, unscaled_ready, u)
                    nc.vector.tensor_reduce(out=total[:], in_=unscaled[:], axis=AX.X, op=ALU.add).then_inc(total_ready, 1)
                    wait_unit(dve, total_ready, u)
                    nc.vector.reciprocal(inv[:], total[:]).then_inc(inv_ready, 1)
                    wait_unit(dve, inv_ready, u)
                    wait_unit(dve, scaled, u - 2, per=SCALED)
                    nc.vector.tensor_tensor(weight[s % 2][:], unscaled[:], inv[:].unsqueeze(2).to_broadcast([P, TILES, E]),
                                            ALU.mult).then_inc(weight_ready, 1)

                def take_weights(u, s):
                    wait_unit(dve, weight_turned, u)
                    wait_unit(dve, bias_product, u - 1)
                    nc.vector.tensor_copy(weightT_parts[0][:], small_turned[:]).then_inc(weightT_ready, 1)
                    wait_count(dve, weightT_ready, u * 2 + 1)
                    nc.vector.tensor_tensor(weightT_parts[1][:], small_turned[:], weightT_parts[0][:], ALU.subtract
                                            ).then_inc(weightT_ready, 1)

                def start_sum(u, s):
                    wait_unit(dve, bias_product, u)
                    wait_unit(dve, upper_summed, u - 2, per=SCALED)
                    nc.vector.tensor_tensor(acc[s % 2][:].rearrange("p t c -> p (t c)"), turned[:],
                                            x_in[s % AHEAD][:].rearrange("p t c -> p (t c)"), ALU.add).then_inc(acc_ready, 1)

                def add_experts(u, s, part):
                    if part == 0:
                        wait_unit(dve, acc_ready, u)
                        wait_unit(dve, weight_ready, u)
                        wait_dma(dve, stored, u - 2, s % 2)
                    for t, e in order[part]:
                        if e == 0:
                            wait_count(dve, low_product, u * TILES + (t + 1))
                        elif e == HALF_E:
                            wait_count(dve, high_product, u * TILES + (t + 1))
                        if e > 0:
                            wait_added(dve, u, t, e - 1)
                        bank = (low if e < HALF_E else high)[t % 2]
                        total_to = out if e == E - 1 else acc
                        nc.vector.scalar_tensor_tensor(
                            total_to[s % 2][:, t, :], bank[:, (e % HALF_E) * C:(e % HALF_E + 1) * C],
                            weight[s % 2][:, t, e:e + 1], acc[s % 2][:, t, :], ALU.mult, ALU.add).then_inc(added, 1)

                for u in range(3):
                    for half in range(2):
                        stats(u, u, half)
                route(0, 0)
                compare(0, 0)
                finish_weights(0, 0)
                take_weights(0, 0)
                start_sum(0, 0)

                def step(u, s):
                    add_experts(u, s, 0)
                    add_experts(u, s, 1)
                    if exists(u + 1, UNITS):
                        route(u + 1, s + 1)
                        compare(u + 1, s + 1)
                    add_experts(u, s, 2)
                    add_experts(u, s, 3)
                    if exists(u + 1, UNITS):
                        finish_weights(u + 1, s + 1)
                    add_experts(u, s, 4)
                    if exists(u + 3, UNITS):
                        stats(u + 3, s + 3, 0)
                    add_experts(u, s, 5)
                    if exists(u + 3, UNITS):
                        stats(u + 3, s + 3, 1)
                    if exists(u + 1, UNITS):
                        take_weights(u + 1, s + 1)
                    add_experts(u, s, 6)
                    add_experts(u, s, 7)
                    if exists(u + 1, UNITS):
                        start_sum(u + 1, s + 1)

                each_unit(dve, UNITS, AHEAD, step)

            @block.gpsimd
            def _(pool):
                def low_part(u, s):
                    wait_unit(pool, high_part, u)
                    wait_unit(pool, high_product, u - 2, per=TILES)
                    nc.gpsimd.tensor_tensor(xT_parts[s % 2][1][:], xT[s % 2][:], xT_parts[s % 2][0][:], ALU.subtract
                                            ).then_inc(parts_ready, 1)

                nc.gpsimd.memset(b_blocks[:], 0.0).then_inc(blocks_zero, 1)
                make_identity(nc, ident, ident_ready)
                norm.prepare(nc)
                g = nc.gpsimd
                g.memset(ones[:], 1.0).then_inc(route_step, 1)
                pool.wait_ge(route_step, 1)

                def norms(u, s):
                    wait_unit(pool, stats_ready, u, per=2)
                    wait_unit(pool, centred_ready, u - 2, per=2)
                    norm.rstd_of(nc, u, s % 2, rstd_ready)

                def choose(u, s):
                    done = [0]

                    def link(instruction):
                        instruction.then_inc(route_step, 1)
                        done[0] += 1
                        wait_count(pool, route_step, u * ROUTE + (done[0] + 1))

                    wait_unit(pool, compared, u)
                    wait_unit(pool, unscaled_ready, u - 1)
                    g.tensor_tensor(places[:], alike[:], ones[:], ALU.add)
                    g.tensor_tensor(rank[0][:, :, 1:E], equal[:, :, 1:E], equal[:, :, 0:E - 1], ALU.add)
                    link(g.tensor_copy(rank[0][:, :, 0:1], equal[:, :, 0:1]))
                    g.tensor_tensor(rank[1][:, :, 2:E], rank[0][:, :, 2:E], rank[0][:, :, 0:E - 2], ALU.add)
                    link(g.tensor_copy(rank[1][:, :, 0:2], rank[0][:, :, 0:2]))
                    g.tensor_tensor(rank[2][:, :, 4:E], rank[1][:, :, 4:E], rank[1][:, :, 0:4], ALU.add)
                    link(g.tensor_copy(rank[2][:, :, 0:4], rank[1][:, :, 0:4]))
                    link(g.tensor_tensor(rank[0][:], rank[2][:], places[:].unsqueeze(2).to_broadcast([P, TILES, E]), ALU.subtract))
                    g.tensor_tensor(wait_tick[:, 0:1], norm.power[:, 0:1], norm.power[:, 0:1], ALU.add)
                    link(g.tensor_scalar(rank[1][:], rank[0][:], 0.0, 0.0, ALU.is_le, ALU.add))
                    link(g.tensor_tensor(rank[0][:], rank[1][:], equal[:], ALU.mult))
                    g.tensor_tensor(chosen[:], first[:], rank[0][:], ALU.add).then_inc(chosen_ready, 1)

                def add_upper(u, s, tiles):
                    for t in tiles:
                        n = SHARED.index(t)
                        wait_scaled(pool, u, t)
                        g.tensor_tensor(pairs[n][:], upper[n][:, 0:2, :], upper[n][:, 2:4, :], ALU.add).then_inc(upper_step, 1)
                        wait_count(pool, upper_step, u * (2 * SCALED) + (2 * n + 1))
                        g.tensor_tensor(upper_sum[n][:], pairs[n][:, 0, :], pairs[n][:, 1, :], ALU.add).then_inc(upper_step, 1)
                        wait_count(pool, upper_step, u * (2 * SCALED) + (2 * n + 2))
                        wait_added(pool, u, t, HALF_E - 1)
                        if n == 0:
                            wait_dma(pool, stored, u - 2, s % 2)
                        g.tensor_tensor(out[s % 2][:, t, :], acc[s % 2][:, t, :], upper_sum[n][:], ALU.add
                                        ).then_inc(upper_summed, 1)

                norms(0, 0)
                norms(1, 1)
                norms(2, 2)
                low_part(0, 0)
                choose(0, 0)

                def step(u, s):
                    if exists(u + 1, UNITS):
                        choose(u + 1, s + 1)
                    add_upper(u, s, SHARED[0:1])
                    if exists(u + 1, UNITS):
                        low_part(u + 1, s + 1)
                    add_upper(u, s, SHARED[1:2])
                    if exists(u + 3, UNITS):
                        norms(u + 3, s + 3)
                    add_upper(u, s, SHARED[2:5])

                each_unit(pool, UNITS, AHEAD, step)

            @block.scalar
            def _(act):
                act.wait_ge(weights_in, loads)

                def take_turned(u, s):
                    wait_unit(act, turned_ready, u)
                    wait_unit(act, high_product, u - 2, per=TILES)
                    wait_unit(act, parts_ready, u - 2)
                    for half in range(2):
                        cols = slice(half * BANK, (half + 1) * BANK)
                        last = nc.scalar.copy(xT[s % 2][:, cols], turned[:, cols])
                    last.then_inc(xT_ready, 1)
                    for half in range(2):
                        cols = slice(half * BANK, (half + 1) * BANK)
                        last = nc.scalar.copy(xT_parts[s % 2][0][:, cols], turned[:, cols])
                    last.then_inc(high_part, 1)

                def centre(u, s, half):
                    wait_unit(act, rstd_ready, u)
                    wait_unit(act, turned_ready, u - 2)
                    norm.apply_on_scalar(nc, s % 2, centred[s % 2], x_in[s % AHEAD], centred_ready,
                                         range(half * TILES // 2, (half + 1) * TILES // 2))

                def shares(u, s):
                    wait_unit(act, shifted_ready, u)
                    wait_unit(act, unscaled_ready, u - 1)
                    nc.scalar.activation(share[:], shifted[:], ACT.Exp).then_inc(exp_ready, 1)

                def scale_upper(u, s, tiles):
                    for t in tiles:
                        n = SHARED.index(t)
                        wait_count(act, high_product, u * TILES + (t + 1))
                        wait_count(act, upper_step, (u - 1) * (2 * SCALED) + (2 * n + 1))
                        if n == 0:
                            wait_unit(act, weight_ready, u)
                        for e in range(HALF_E):
                            last = nc.scalar.activation(upper[n][:, e, :], high[t % 2][:, e * C:(e + 1) * C], ACT.Copy,
                                                        scale=weight[s % 2][:, t, HALF_E + e:HALF_E + e + 1])
                        last.then_inc(scaled, 1)

                def store(u, s):
                    wait_unit(act, upper_summed, u, per=SCALED)
                    wait_unit(act, added, u, per=ADDED)
                    act.dma_start(x4_units[u], out[s % 2][:]).then_inc(stored[s % 2], 16)

                for u in range(2):
                    for half in range(2):
                        centre(u, u, half)
                take_turned(0, 0)
                shares(0, 0)

                def step(u, s):
                    scale_upper(u, s, SHARED[0:1])
                    if exists(u + 1, UNITS):
                        take_turned(u + 1, s + 1)
                    scale_upper(u, s, SHARED[1:2])
                    if exists(u - 1, UNITS):
                        store(u - 1, s + 1)
                    if exists(u + 1, UNITS):
                        shares(u + 1, s + 1)
                    if exists(u + 2, UNITS):
                        centre(u + 2, s + 2, 0)
                    scale_upper(u, s, SHARED[2:3])
                    if exists(u + 2, UNITS):
                        centre(u + 2, s + 2, 1)
                    scale_upper(u, s, SHARED[3:5])

                each_unit(act, UNITS, AHEAD, step)
                store(UNITS - 1, UNITS - 1)
                for s in range(2):
                    wait_dma(act, stored, UNITS - 2 + s, s)

        mem.clear()


def two_metaformer_layers(nc, a, out):
    def scratch(name, shape):
        return nc.dram_tensor(name, shape, F32, kind="Internal").ap()

    normed = scratch("normed", [ROWS, C, COLS])
    pair_bias = scratch("pair_bias", [HEADS, ROWS, COLS])
    x1, x2, x3 = (scratch(n, [TOKENS, C]) for n in ("x1", "x2", "x3"))
    wx, y, out_gate = (scratch(n, [UNITS, C, UNIT]) for n in ("wx", "y", "out_gate"))
    left, right, tri = (scratch(n, [C, PITCH]) for n in ("left", "right", "tri"))
    x = a["x"].rearrange("b i j c -> (b i j) c")
    x4 = out.rearrange("b i j c -> (b i j) c")
    bias_rows = pair_bias.rearrange("h j k -> h (j k)")
    l0, l1 = "L0_conv_", "L1_conv_"

    norm_project(nc, "norm", x, a[l0 + "Wb"], a[l0 + "ln_gamma"], a[l0 + "ln_beta"], normed,
                 lambda u: bias_rows[:, bass.ds(u * UNIT, UNIT)], HEADS, 1 + EPS_LN, EPS_C * EPS_LN)
    attention(nc, x, normed, pair_bias, *(a[l0 + n] for n in ("Wq", "Wk", "Wv", "Wg", "bg", "Wo", "bo")), x1)
    with nc.sbuf_tensor("wx_stats", [C, 2], F32) as wx_stats:
        norm_project(nc, "mix", x1, a["L0_ffn_W"], None, None, None, lambda u: wx[u], C, 1.0, EPS_T, wx_stats)
        recurrence(nc, wx, wx_stats, a["L0_ffn_V"], a["L0_ffn_gamma"], a["L0_ffn_beta"], y)
    names = ("lgate", "left", "rgate", "right", "ogate")
    gates(nc, x1, y, a[l1 + "norm_g"], a[l1 + "norm_b"], [a[l1 + n + "_w"] for n in names],
          [a[l1 + n + "_b"] for n in names], x2, left, right, out_gate)
    triangle(nc, left, right, tri)
    triangle_out(nc, tri, out_gate, x2, a[l1 + "onorm_g"], a[l1 + "onorm_b"], a[l1 + "to_out_w"], a[l1 + "to_out_b"], x3)
    experts(nc, x3, *(a["L1_ffn_" + n] for n in ("router_w", "router_b", "expert_w", "expert_b")), x4)


def kernel(**inputs):
    import concourse.bacc as bacc
    from concourse.bass_utils import run_bass_kernel_spmd

    nc = bacc.Bacc("TRN2", target_bir_lowering=False, num_devices=1)
    arrays, aps = {}, {}
    for name, value in inputs.items():
        value = np.ascontiguousarray(value)
        arrays[name] = value
        aps[name] = nc.dram_tensor(name, value.shape, mybir.dt.from_np(value.dtype), kind="ExternalInput").ap()
    out = nc.dram_tensor("x_out", inputs["x"].shape, F32, kind="ExternalOutput").ap()
    two_metaformer_layers(nc, aps, out)
    result = run_bass_kernel_spmd(nc, [arrays], core_ids=[0])
    return result.results[0]["x_out"]
```
